# Optimizing a Trainium2 kernel written in Bass

```python
import numpy as np
import jax
import jax.numpy as jnp

def _softmax(x, axis=-1):
    return jax.nn.softmax(x, axis=axis)

def _gelu(x):
    return jax.nn.gelu(x, approximate=True)

def _silu(x):
    return jax.nn.silu(x)

def _sigmoid(x):
    return jax.nn.sigmoid(x)

def _layernorm(x, axis=-1, eps=1e-05):
    m = jnp.mean(x, axis=axis, keepdims=True)
    v = jnp.var(x, axis=axis, keepdims=True)
    return (x - m) / jnp.sqrt(v + eps)

def _scatter_add(tgt, idx, src, axis=0):
    return tgt.at[idx].add(src)

def _segment_sum(src, seg, n):
    return jax.ops.segment_sum(src, seg, n)
kernel_name = 'mk_recurrent_d2_jaxref_r8_71ac75'

def setup_inputs(seed: int=0):
    np.random.seed(seed)
    _w = jnp.asarray

    def _L0_attn_setup():
        import jax, jax.numpy as jnp
        from jax import lax
        import numpy as np
        D_MODEL, D_INNER, D_STATE, D_CONV, DT_RANK = (128, 256, 16, 4, 64)
        B, L = (2, 128)
        key = jax.random.key(seed)
        ks = jax.random.split(key, 10)
        s = lambda *sh: 1.0 / np.sqrt(sh[0])
        return {'x': jax.random.normal(ks[0], (B, L, D_MODEL), jnp.float32), 'W_in': jax.random.normal(ks[1], (D_MODEL, 2 * D_INNER), jnp.float32) * s(D_MODEL), 'conv_w': jax.random.normal(ks[2], (D_INNER, D_CONV), jnp.float32) * s(D_CONV), 'conv_b': jax.random.normal(ks[3], (D_INNER,), jnp.float32) * 0.1, 'W_x': jax.random.normal(ks[4], (D_INNER, DT_RANK + 2 * D_STATE), jnp.float32) * s(D_INNER), 'W_dt': jax.random.normal(ks[5], (DT_RANK, D_INNER), jnp.float32) * s(DT_RANK), 'b_dt': jax.random.uniform(ks[6], (D_INNER,), jnp.float32, -4.0, -2.0), 'A_log': jnp.log(jnp.broadcast_to(jnp.arange(1, D_STATE + 1, dtype=jnp.float32), (D_INNER, D_STATE))), 'D_param': jnp.ones((D_INNER,), jnp.float32), 'W_out': jax.random.normal(ks[7], (D_INNER, D_MODEL), jnp.float32) * s(D_INNER)}
    _L0_attn_in = _L0_attn_setup()

    def _L0_ffn_setup():
        import jax, jax.numpy as jnp
        import numpy as np
        DIM = 128
        HIDDEN = 512
        E = 8
        K = 2

        def _ffn_hidden(h, multiple_of=32):
            h = int(2 * h / 3)
            return multiple_of * ((h + multiple_of - 1) // multiple_of)
        EXP_HID = _ffn_hidden(HIDDEN)
        SH_HID = _ffn_hidden(HIDDEN // 2)

        def _swiglu(t, a, b, c):
            return jax.nn.silu(t @ a) * (t @ c) @ b
        key = jax.random.key(seed)
        ks = jax.random.split(key, 8)

        def xavier(k, shape, fan_in, fan_out):
            lim = np.sqrt(6.0 / (fan_in + fan_out)).astype(np.float32)
            return jax.random.uniform(k, shape, jnp.float32, -lim, lim)
        return {'x': jax.random.normal(ks[0], (2, 256, DIM), jnp.float32), 'gate_w': xavier(ks[1], (E, DIM), DIM, E), 'w1': xavier(ks[2], (E, DIM, EXP_HID), DIM, EXP_HID), 'w2': xavier(ks[3], (E, EXP_HID, DIM), EXP_HID, DIM), 'w3': xavier(ks[4], (E, DIM, EXP_HID), DIM, EXP_HID), 'sw1': xavier(ks[5], (DIM, SH_HID), DIM, SH_HID), 'sw2': xavier(ks[6], (SH_HID, DIM), SH_HID, DIM), 'sw3': xavier(ks[7], (DIM, SH_HID), DIM, SH_HID)}
    _L0_ffn_in = _L0_ffn_setup()

    def _L1_attn_setup():
        import jax, jax.numpy as jnp
        import numpy as np
        key = jax.random.key(seed)
        k1, k2, k3 = jax.random.split(key, 3)
        bs, seqlen, hidden = (2, 256, 128)
        s, h = (4, 32)
        std = 0.02
        num_layers = 12
        hidden_states = jax.random.normal(k1, (bs, seqlen, hidden), dtype=jnp.float32)
        q_scale = 1.0 / np.sqrt(2.0 * num_layers * h)
        queries = jax.random.normal(k2, (s, h, h * s), dtype=jnp.float32) * std * q_scale
        combiners = jax.random.normal(k3, (s, h * s, h), dtype=jnp.float32) * (std * q_scale)
        return {'hidden_states': hidden_states, 'queries': queries, 'combiners': combiners}
    _L1_attn_in = _L1_attn_setup()

    def _L1_ffn_setup():
        import jax, jax.numpy as jnp
        import numpy as np
        B, S, H = (2, 512, 128)
        E, K, I = (8, 2, 176)
        key = jax.random.key(seed)
        ks = jax.random.split(key, 9)
        sc = 0.02
        return {'hidden_states': jax.random.normal(ks[0], (B, S, H), jnp.float32), 'gate_w': jax.random.normal(ks[1], (E, H), jnp.float32) * sc, 'w_gate': jax.random.normal(ks[2], (E, H, I), jnp.float32) * sc, 'w_up': jax.random.normal(ks[3], (E, H, I), jnp.float32) * sc, 'w_down': jax.random.normal(ks[4], (E, I, H), jnp.float32) * sc, 'sw_gate': jax.random.normal(ks[5], (H, I), jnp.float32) * sc, 'sw_up': jax.random.normal(ks[6], (H, I), jnp.float32) * sc, 'sw_down': jax.random.normal(ks[7], (I, H), jnp.float32) * sc, 'shared_gate_w': jax.random.normal(ks[8], (1, H), jnp.float32) * sc}
    _L1_ffn_in = _L1_ffn_setup()
    _d = {'L0_attn_x': _L0_attn_in['x'], 'L0_attn_W_in': _L0_attn_in['W_in'], 'L0_attn_conv_w': _L0_attn_in['conv_w'], 'L0_attn_conv_b': _L0_attn_in['conv_b'], 'L0_attn_W_x': _L0_attn_in['W_x'], 'L0_attn_W_dt': _L0_attn_in['W_dt'], 'L0_attn_b_dt': _L0_attn_in['b_dt'], 'L0_attn_A_log': _L0_attn_in['A_log'], 'L0_attn_D_param': _L0_attn_in['D_param'], 'L0_attn_W_out': _L0_attn_in['W_out'], 'L0_ffn_gate_w': _L0_ffn_in['gate_w'], 'L0_ffn_w1': _L0_ffn_in['w1'], 'L0_ffn_w2': _L0_ffn_in['w2'], 'L0_ffn_w3': _L0_ffn_in['w3'], 'L0_ffn_sw1': _L0_ffn_in['sw1'], 'L0_ffn_sw2': _L0_ffn_in['sw2'], 'L0_ffn_sw3': _L0_ffn_in['sw3'], 'L1_attn_queries': _L1_attn_in['queries'], 'L1_attn_combiners': _L1_attn_in['combiners'], 'L1_ffn_gate_w': _L1_ffn_in['gate_w'], 'L1_ffn_w_gate': _L1_ffn_in['w_gate'], 'L1_ffn_w_up': _L1_ffn_in['w_up'], 'L1_ffn_w_down': _L1_ffn_in['w_down'], 'L1_ffn_sw_gate': _L1_ffn_in['sw_gate'], 'L1_ffn_sw_up': _L1_ffn_in['sw_up'], 'L1_ffn_sw_down': _L1_ffn_in['sw_down'], 'L1_ffn_shared_gate_w': _L1_ffn_in['shared_gate_w']}
    _x0 = _d['L0_attn_x']
    _d['L0_attn_x'] = jax.random.normal(jax.random.fold_in(jax.random.key(seed), 1), (4, 1024, 128), dtype=_x0.dtype)
    del _x0
    return _d

def reference(L0_attn_x, L0_attn_W_in, L0_attn_conv_w, L0_attn_conv_b, L0_attn_W_x, L0_attn_W_dt, L0_attn_b_dt, L0_attn_A_log, L0_attn_D_param, L0_attn_W_out, L0_ffn_gate_w, L0_ffn_w1, L0_ffn_w2, L0_ffn_w3, L0_ffn_sw1, L0_ffn_sw2, L0_ffn_sw3, L1_attn_queries, L1_attn_combiners, L1_ffn_gate_w, L1_ffn_w_gate, L1_ffn_w_up, L1_ffn_w_down, L1_ffn_sw_gate, L1_ffn_sw_up, L1_ffn_sw_down, L1_ffn_shared_gate_w):

    def _L0_attn_ref(x, W_in, conv_w, conv_b, W_x, W_dt, b_dt, A_log, D_param, W_out):
        import jax, jax.numpy as jnp
        from jax import lax
        import numpy as np
        D_MODEL, D_INNER, D_STATE, D_CONV, DT_RANK = (128, 256, 16, 4, 64)
        B, L = (2, 128)
        b, l, _ = x.shape
        d_inner, d_conv = conv_w.shape
        dt_rank = W_dt.shape[0]
        d_state = A_log.shape[1]
        xz = x @ W_in
        xs, z = jnp.split(xz, 2, axis=-1)
        xp = jnp.pad(xs, ((0, 0), (d_conv - 1, 0), (0, 0))).transpose(0, 2, 1)
        xc = lax.conv_general_dilated(xp, conv_w[:, None, :], (1,), 'VALID', feature_group_count=d_inner, dimension_numbers=('NCH', 'OIH', 'NCH'))
        xc = jax.nn.silu(xc.transpose(0, 2, 1) + conv_b)
        dbl = xc @ W_x
        dt = jax.nn.softplus(dbl[..., :dt_rank] @ W_dt + b_dt)
        Bm = dbl[..., dt_rank:dt_rank + d_state]
        Cm = dbl[..., dt_rank + d_state:]
        A = -jnp.exp(A_log)
        dA = jnp.exp(dt[..., None] * A)
        dBx = (dt * xc)[..., None] * Bm[:, :, None, :]

        def step(h, inp):
            dA_t, dBx_t, C_t = inp
            h = dA_t * h + dBx_t
            y = jnp.einsum('bdn,bn->bd', h, C_t)
            return (h, y)
        h0 = jnp.zeros((b, d_inner, d_state), x.dtype)
        _, ys = lax.scan(step, h0, (dA.transpose(1, 0, 2, 3), dBx.transpose(1, 0, 2, 3), Cm.transpose(1, 0, 2)))
        y = ys.transpose(1, 0, 2) + xc * D_param
        y = y * jax.nn.silu(z)
        return y @ W_out

    def _L0_ffn_ref(x, gate_w, w1, w2, w3, sw1, sw2, sw3):
        import jax, jax.numpy as jnp
        import numpy as np
        DIM = 128
        HIDDEN = 512
        E = 8
        K = 2

        def _ffn_hidden(h, multiple_of=32):
            h = int(2 * h / 3)
            return multiple_of * ((h + multiple_of - 1) // multiple_of)
        EXP_HID = _ffn_hidden(HIDDEN)
        SH_HID = _ffn_hidden(HIDDEN // 2)

        def _swiglu(t, a, b, c):
            return jax.nn.silu(t @ a) * (t @ c) @ b
        B, S, D = x.shape
        xt = x.reshape(-1, D)
        T = xt.shape[0]
        logits = xt @ gate_w.T
        scores = jax.nn.softmax(logits, axis=-1)
        topk_w, topk_i = jax.lax.top_k(scores, K)
        comb = jnp.zeros((T, E), x.dtype).at[jnp.arange(T)[:, None], topk_i].add(topk_w)
        y = jnp.zeros_like(xt)
        for e in range(E):
            y = y + comb[:, e:e + 1] * _swiglu(xt, w1[e], w2[e], w3[e])
        y = y.reshape(B, S, D)
        return y + _swiglu(x, sw1, sw2, sw3)

    def _L1_attn_ref(hidden_states, queries, combiners):
        import jax, jax.numpy as jnp
        import numpy as np
        s, h, _ = queries.shape
        bs, S, E = hidden_states.shape
        x = hidden_states.reshape(bs, S, s, h)
        qw = queries.reshape(s, h, s, h)
        Q = jnp.einsum('btae,aeqf->qbtaf', x, qw)
        pre = jnp.einsum('qbtaf,buqf->qbtau', Q, x)
        attn = jnp.einsum('qbtau,buqg->abtqg', pre, x)
        attn = attn.reshape(s, bs, S, s * h)
        out = jnp.einsum('abtk,akg->btag', attn, combiners)
        return out.reshape(bs, S, s * h)

    def _L1_ffn_ref(hidden_states, gate_w, w_gate, w_up, w_down, sw_gate, sw_up, sw_down, shared_gate_w):
        import jax, jax.numpy as jnp
        import numpy as np
        B, S, H = (2, 512, 128)
        E, K, I = (8, 2, 176)
        b, s, h = hidden_states.shape
        x = hidden_states.reshape(-1, h)
        logits = jnp.einsum('th,eh->te', x, gate_w)
        probs = jax.nn.softmax(logits.astype(jnp.float32), axis=-1)
        topk_w, topk_i = jax.lax.top_k(probs, K)
        topk_w = topk_w / jnp.sum(topk_w, axis=-1, keepdims=True)
        combine = jnp.sum(jax.nn.one_hot(topk_i, E, dtype=topk_w.dtype) * topk_w[..., None], axis=1)
        combine = combine.astype(x.dtype)
        g = jnp.einsum('th,ehi->eti', x, w_gate)
        u = jnp.einsum('th,ehi->eti', x, w_up)
        eo = jnp.einsum('eti,eih->eth', jax.nn.silu(g) * u, w_down)
        out = jnp.einsum('te,eth->th', combine, eo)
        sg = jax.nn.sigmoid(jnp.einsum('th,oh->to', x, shared_gate_w))
        so = jax.nn.silu(x @ sw_gate) * (x @ sw_up) @ sw_down
        out = out + sg * so
        return out.reshape(b, s, h)
    x = L0_attn_x
    xn = _layernorm(x, axis=-1)
    s = _L0_attn_ref(xn, L0_attn_W_in, L0_attn_conv_w, L0_attn_conv_b, L0_attn_W_x, L0_attn_W_dt, L0_attn_b_dt, L0_attn_A_log, L0_attn_D_param, L0_attn_W_out)
    g = _silu(_L0_ffn_ref(xn, L0_ffn_gate_w, L0_ffn_w1, L0_ffn_w2, L0_ffn_w3, L0_ffn_sw1, L0_ffn_sw2, L0_ffn_sw3))
    x = x + s * g
    xn = _layernorm(x, axis=-1)
    s = _L1_attn_ref(xn, L1_attn_queries, L1_attn_combiners)
    g = _silu(_L1_ffn_ref(xn, L1_ffn_gate_w, L1_ffn_w_gate, L1_ffn_w_up, L1_ffn_w_down, L1_ffn_sw_gate, L1_ffn_sw_up, L1_ffn_sw_down, L1_ffn_shared_gate_w))
    x = x + s * g
    return x

_drawn_inputs = setup_inputs


def setup_inputs(seed=0):
    import zlib

    import numpy as np

    out = dict(_drawn_inputs(seed))
    spreads = {'L0_attn_D_param': (1.0, 0.6)}
    factors = {'L0_attn_conv_b': 4.207,
     'L0_attn_W_dt': 3.421,
     'L0_attn_b_dt': 4.607,
     'L0_attn_A_log': 2.745,
     'L1_attn_queries': 8.0,
     'L1_attn_combiners': 8.0,
     'L1_ffn_gate_w': 8.0,
     'L1_ffn_w_gate': 8.0,
     'L1_ffn_w_up': 8.0,
     'L1_ffn_w_down': 8.0,
     'L1_ffn_sw_gate': 8.0,
     'L1_ffn_sw_up': 8.0,
     'L1_ffn_sw_down': 8.0,
     'L1_ffn_shared_gate_w': 8.0}
    for name, (base, spread) in spreads.items():
        noise = np.random.default_rng([zlib.crc32(name.encode()), seed]).standard_normal(out[name].shape)
        drawn = base * np.exp(spread * noise) if base else spread * noise
        out[name] = jnp.asarray(drawn.astype(out[name].dtype))
    for name, factor in factors.items():
        out[name] = (out[name] * factor).astype(out[name].dtype)
    return out
```

```python
from contextlib import ExitStack

import concourse.bass as bass
from concourse import mybir

F32 = mybir.dt.float32
U32 = mybir.dt.uint32
ALU = mybir.AluOpType
ACT = mybir.ActivationFunctionType
AX = mybir.AxisListType.X

P = 128
NB, L = 4, 1024
CT = L // P
HALF = 512
NS = 16
DI = 256
DK = DI // P
R = 64
NE = 8
H0 = 352
S0 = 192
H1 = 176
K0 = [128, 128, 96]
K0S = [128, 64]
K1 = [128, 48]
GB = 2
EPS = 1e-5


def program(nc, T, out):
    with ExitStack() as ctx:
        def sb(name, shape, dt=F32):
            return ctx.enter_context(nc.sbuf_tensor(name, shape, dt))

        def sem(name):
            return ctx.enter_context(nc.semaphore(name))

        w13a = sb("w13a", [P, NE, 2 * H0])
        w2a = sb("w2a", [P, NE, 3, P])
        w13s = sb("w13s", [P, 2 * S0])
        w2s = sb("w2s", [P, 2, P])
        w13b = sb("w13b", [P, NE + 1, 2 * H1])
        w2b = sb("w2b", [P, NE + 1, 2, P])
        w_in = sb("w_in", [P, 2 * DI])
        w_x = sb("w_x", [P, DK, R + 2 * NS])
        w_dt = sb("w_dt", [R, DI])
        w_out = sb("w_out", [P, DK, P])
        cw = sb("cw", [P, DK, 4])
        cb = sb("cb", [P, DK])
        bdt = sb("bdt", [P, DK])
        am = sb("am", [P, DK, NS])
        dpar = sb("dpar", [P, DK])
        gate = [sb("gate0", [P, NE]), sb("gate1", [P, NE + 1])]
        combi = sb("combi", [P, P])
        queryT = sb("queryT", [P, P])
        ident = sb("ident", [P, P])
        iota8 = sb("iota8", [P, NE])
        mhalf = sb("mhalf", [P, CT])

        x = sb("x", [P, CT, P])
        xn = sb("xn", [P, CT, P])
        xnT = sb("xnT", [P, L])
        moe = sb("moe", [P, CT, P])
        s_sb = sb("s_sb", [P, CT, P])
        tg = sb("tg", [P, CT, P])
        stats = sb("stats", [P, CT, 6])
        mv = sb("mv", [P, CT, 2])
        vpe = sb("vpe", [P, CT])
        rstd = sb("rstd", [P, CT])
        mx = sb("mx", [P, CT])
        zl = sb("zl", [P, CT, NE])
        el = sb("el", [P, CT, NE])
        se = sb("se", [P, CT])
        pr = sb("pr", [P, CT, NE])
        top = sb("top", [P, CT, 8])
        idx = sb("idx", [P, CT, 8], U32)
        idf = sb("idf", [P, CT, 2])
        wk = sb("wk", [P, CT, 2])
        oh = sb("oh", [P, 2, CT, NE])
        tsg = sb("tsg", [P, CT])
        comb = sb("comb", [P, CT, NE + 1])
        bd = sb("bd", [P, P])
        pm = sb("pm", [P, P])
        bdw = sb("bdw", [P, P])

        xs = sb("xs", [P, DK, HALF + 3])
        ca = sb("ca", [P, DK, HALF])
        th = sb("th", [P, DK, HALF])
        xc = sb("xc", [P, DK, HALF])
        zs = sb("zs", [P, DK, HALF])
        dbl = sb("dbl", [R + 2 * NS, HALF])
        v = sb("v", [P, DK, HALF])
        ea = sb("ea", [P, DK, HALF])
        ln = sb("ln", [P, DK, HALF])
        dt = sb("dt", [P, DK, HALF])
        dtx = sb("dtx", [P, DK, HALF])
        y = sb("y", [P, DK, HALF])
        carry = sb("carry", [P, DK, NS])
        bcb = sb("bcb", [P, 2, GB, HALF])
        bcc = sb("bcc", [P, 2, GB, HALF])
        dA = sb("dA", [P, 2, DK, HALF])
        dBx = sb("dBx", [P, 2, DK, HALF])
        h = sb("h", [P, 2, DK, HALF])
        g = sb("g", [P, DK, HALF])
        tj = sb("tj", [P, 2, H0])
        aj = sb("aj", [P, 2, H0])
        hj = sb("hj", [P, 2, H0])
        hT = sb("hT", [P, 2, 3 * P])

        bc_dram = nc.dram_tensor("bc_rows", (2 * NB, 2 * NS, HALF), F32, kind="Internal").ap()

        pG = ctx.enter_context(nc.psum_tensor("pG", [P, 2, 512], F32))
        pU = ctx.enter_context(nc.psum_tensor("pU", [P, 2, 512], F32))
        pT = ctx.enter_context(nc.psum_tensor("pT", [P, 2, 512], F32))
        pM = ctx.enter_context(nc.psum_tensor("pM", [P, 2, 512], F32))

        loaded = sem("loaded")
        mixer_loaded = sem("mixer_loaded")
        x_in = sem("x_in")
        out_stored = sem("out_stored")
        ident_ready = sem("ident_ready")
        const_ready = sem("const_ready")
        consts_ready = sem("consts_ready")
        scaled = sem("scaled")
        stats_ready = sem("stats_ready")
        ve_ready = sem("ve_ready")
        rstd_ready = sem("rstd_ready")
        xn_ready = sem("xn_ready")
        xnT_pe = sem("xnT_pe")
        xnT_copied = sem("xnT_copied")
        logits_pe = sem("logits_pe")
        zl_ready = sem("zl_ready")
        el_ready = sem("el_ready")
        tsg_ready = sem("tsg_ready")
        in_pe = sem("in_pe")
        xs_copied = sem("xs_copied")
        th_ready = sem("th_ready")
        conv_ready = sem("conv_ready")
        thc_ready = sem("thc_ready")
        xc_ready = sem("xc_ready")
        dbl_pe = sem("dbl_pe")
        dbl_copied = sem("dbl_copied")
        rows_stored = sem("rows_stored")
        dtr_pe = sem("dtr_pe")
        v_ready = sem("v_ready")
        ln_ready = sem("ln_ready")
        dt_ready = sem("dt_ready")
        dtx_ready = sem("dtx_ready")
        dA_ready = sem("dA_ready")
        dBx_ready = sem("dBx_ready")
        h_ready = sem("h_ready")
        carried = sem("carried")
        g_ready = sem("g_ready")
        y2_ready = sem("y2_ready")
        out_pe = sem("out_pe")
        s_copied = sem("s_copied")
        gram_pe = sem("gram_pe")
        bd_ready = sem("bd_ready")
        pm_pe = sem("pm_pe")
        pm_ready = sem("pm_ready")
        w_pe = sem("w_pe")
        bdw_ready = sem("bdw_ready")
        attn_pe = sem("attn_pe")
        gu_ready = sem("gu_ready")
        tanh_ready = sem("tanh_ready")
        a_ready = sem("a_ready")
        hj_ready = sem("hj_ready")
        hT_pe = sem("hT_pe")
        hT_copied = sem("hT_copied")
        y_pe = sem("y_pe")
        y_used = sem("y_used")
        x_out = sem("x_out")
        chain = sem("chain")
        tg_ready = sem("tg_ready")
        bc_loaded = [sem("bc_loaded0"), sem("bc_loaded1")]

        block = ctx.enter_context(nc.Block())
        JOBS = CT * (NE + 1)
        CH = 2 * NB

        mixer_loads = [
            (x[:], None),
            (w_in[:], T["L0_attn_W_in"]),
            (w_x[:], T["L0_attn_W_x"].rearrange("(k p) n -> p k n", p=P)),
            (w_dt[:], T["L0_attn_W_dt"]),
            (w_out[:], T["L0_attn_W_out"].rearrange("(k p) n -> p k n", p=P)),
            (cw[:], T["L0_attn_conv_w"].rearrange("(k p) j -> p k j", p=P)),
            (cb[:], T["conv_b"]), (bdt[:], T["b_dt"]), (dpar[:], T["D_param"]),
            (am[:], T["L0_attn_A_log"].rearrange("(k p) n -> p k n", p=P)),
            (gate[0][:], T["gate0T"]), (gate[1][:], T["gate1T"]),
            (combi[:], T["combi"]), (queryT[:], T["queryT"]),
        ][1:]
        w1, w3, w2 = T["L0_ffn_w1"], T["L0_ffn_w3"], T["L0_ffn_w2"]
        v1, v3, v2 = T["L1_ffn_w_gate"], T["L1_ffn_w_up"], T["L1_ffn_w_down"]
        expert_loads = [
            (w13a[:, :, 0:H0], w1.rearrange("e d h -> d e h")),
            (w13a[:, :, H0:2 * H0], w3.rearrange("e d h -> d e h")),
            (w2a[:, :, 0, :], w2[:, 0:128, :].rearrange("e h d -> h e d")),
            (w2a[:, :, 1, :], w2[:, 128:256, :].rearrange("e h d -> h e d")),
            (w2a[0:96, :, 2, :], w2[:, 256:352, :].rearrange("e h d -> h e d")),
            (w13s[:, 0:S0], T["L0_ffn_sw1"]), (w13s[:, S0:2 * S0], T["L0_ffn_sw3"]),
            (w2s[:, 0, :], T["L0_ffn_sw2"][0:128, :]), (w2s[0:64, 1, :], T["L0_ffn_sw2"][128:192, :]),
            (w13b[:, 0:NE, 0:H1], v1.rearrange("e d h -> d e h")),
            (w13b[:, 0:NE, H1:2 * H1], v3.rearrange("e d h -> d e h")),
            (w13b[:, NE, 0:H1], T["L1_ffn_sw_gate"]), (w13b[:, NE, H1:2 * H1], T["L1_ffn_sw_up"]),
            (w2b[:, 0:NE, 0, :], v2[:, 0:128, :].rearrange("e h d -> h e d")),
            (w2b[0:48, 0:NE, 1, :], v2[:, 128:176, :].rearrange("e h d -> h e d")),
            (w2b[:, NE, 0, :], T["L1_ffn_sw_down"][0:128, :]), (w2b[0:48, NE, 1, :], T["L1_ffn_sw_down"][128:176, :]),
        ]
        N_MIX, N_EXP = 16 * len(mixer_loads), 16 * len(expert_loads)

        @block.sync
        def _(sp):
            for b in range(NB):
                if b:
                    sp.wait_ge(out_stored, 16 * b)
                sp.dma_start(x[:], T["L0_attn_x"][b].rearrange("(c p) d -> p c d", p=P)).then_inc(x_in, 16)
                if b == 0:
                    for dst, src in mixer_loads:
                        sp.dma_start(dst, src).then_inc(mixer_loaded, 16)
                    for dst, src in expert_loads:
                        sp.dma_start(dst, src).then_inc(loaded, 16)
                for q in (2 * b, 2 * b + 1):
                    sp.wait_ge(dbl_copied, q + 1)
                    sp.dma_start(bc_dram[q], dbl[R:R + 2 * NS, :]).then_inc(rows_stored, 16)
                    sp.wait_ge(rows_stored, 16 * (q + 1))
                    for gi in range(NS // GB):
                        if (NS // GB) * q + gi >= 2:
                            sp.wait_ge(dBx_ready, GB * ((NS // GB) * q + gi - 1))
                            sp.wait_ge(g_ready, GB * ((NS // GB) * q + gi - 1))
                        for k, ring in enumerate((bcb, bcc)):
                            src = bc_dram[q, k * NS + gi * GB:k * NS + gi * GB + GB, :]
                            sp.dma_start(ring[:, gi % 2, :, :], src.rearrange("(o n) t -> o n t", o=1).broadcast_to([P, GB, HALF])
                                         ).then_inc(bc_loaded[gi % 2], 16)
                sp.wait_ge(x_out, b + 1)
                sp.dma_start(out[b].rearrange("(c p) d -> p c d", p=P), x[:]).then_inc(out_stored, 16)
            sp.wait_ge(out_stored, 16 * NB)

        @block.gpsimd
        def _(pool):
            pool.memset(ident[:], 0.0).then_inc(const_ready, 1)
            pool.wait_ge(const_ready, 1)
            pool.affine_select(out=ident[:], in_=ident[:], compare_op=ALU.not_equal, fill=1.0, base=0,
                               pattern=[[-1, P]], channel_multiplier=1).then_inc(ident_ready, 1)
            for e in range(NE):
                pool.memset(iota8[:, e:e + 1], float(e))
            pool.memset(mhalf[:], -0.5).then_inc(consts_ready, 1)
            pool.wait_ge(consts_ready, 1)

            def norm(i):
                pool.wait_ge(stats_ready, i + 1)
                pool.tensor_scalar(vpe[:], mv[:, :, 1], EPS, None, ALU.add).then_inc(ve_ready, 1)
                pool.wait_ge(ve_ready, i + 1)
                pool.tensor_tensor(rstd[:], vpe[:], mhalf[:], ALU.pow).then_inc(rstd_ready, 1)

            for b in range(NB):
                norm(2 * b)
                for q in (2 * b, 2 * b + 1):
                    pool.wait_ge(dtx_ready, q + 1)
                    for n in range(NS):
                        N = q * NS + n
                        if n % GB == 0:
                            pool.wait_ge(bc_loaded[n // GB % 2], 32 * (((NS // GB) * q + n // GB) // 2 + 1))
                        if N >= 2:
                            pool.wait_ge(h_ready, 2 * (N - 1))
                        pool.tensor_tensor(dBx[:, n % 2], dtx[:],
                                           bcb[:, n // GB % 2, n % GB:n % GB + 1, :].broadcast_to([P, DK, HALF]),
                                           ALU.mult).then_inc(dBx_ready, 1)
                norm(2 * b + 1)

        @block.tensor
        def _(pe):
            mm = pe.matmul

            def front(b, l):
                i = 2 * b + l
                pe.wait_ge(xn_ready, i + 1)
                if i == 0:
                    pe.wait_ge(ident_ready, 1)
                for c in range(CT):
                    last = pe.transpose(pM[:, c // 4, (c % 4) * P:(c % 4 + 1) * P], xn[:, c, :], ident[:])
                    if c % 4 == 3:
                        last.then_inc(xnT_pe, 1)
                pe.wait_ge(xnT_copied, 2 * (i + 1))
                if i == 0:
                    pe.wait_ge(mixer_loaded, N_MIX)
                for c in range(CT):
                    last = mm(pM[:, 0, 16 * c:16 * c + NE + l], xnT[:, c * P:(c + 1) * P], gate[l][:], start=True, stop=True)
                last.then_inc(logits_pe, 1)

            def mixer(b):
                for q in (2 * b, 2 * b + 1):
                    t0 = (q % 2) * HALF
                    if q % 2 == 0:
                        pe.wait_ge(zl_ready, 2 * b + 1)
                    else:
                        pe.wait_ge(s_copied, 2 * b + b + 1)
                    for m in range(4):
                        if m == 2:
                            pe.wait_ge(xs_copied, 2 * (q + 1) - 1)
                        if m == 3:
                            pe.wait_ge(xs_copied, 2 * (q + 1))
                        mm(pM[:, m % 2, :], w_in[:, m * P:(m + 1) * P], xnT[:, t0:t0 + HALF], start=True, stop=True
                           ).then_inc(in_pe, 1)
                    pe.wait_ge(xc_ready, 2 * (q + 1))
                    for k in range(DK):
                        last = mm(pM[0:R + 2 * NS, 0, :], w_x[:, k, :], xc[:, k, :], start=(k == 0), stop=(k == DK - 1))
                    last.then_inc(dbl_pe, 1)
                    pe.wait_ge(dbl_copied, q + 1)
                    for k in range(DK):
                        mm(pM[:, 1 - k, :], w_dt[:, k * P:(k + 1) * P], dbl[0:R, :], start=True, stop=True
                           ).then_inc(dtr_pe, 1)
                    pe.wait_ge(y2_ready, q + 1)
                    for c in range(4):
                        for k in range(DK):
                            last = mm(pM[:, 1, c * P:(c + 1) * P], y[:, k, c * P:(c + 1) * P], w_out[:, k, :],
                                      start=(k == 0), stop=(k == DK - 1))
                    last.then_inc(out_pe, 1)

            def attn(b):
                pe.wait_ge(zl_ready, 2 * b + 2)
                pe.wait_ge(tsg_ready, b + 1)
                for c in range(CT):
                    last = mm(pM[:, 0, 0:P], xn[:, c, :], xn[:, c, :], start=(c == 0), stop=(c == CT - 1))
                last.then_inc(gram_pe, 1)
                pe.wait_ge(bd_ready, b + 1)
                mm(pM[:, 0, P:2 * P], bd[:], combi[:], start=True, stop=True).then_inc(pm_pe, 1)
                pe.wait_ge(pm_ready, b + 1)
                mm(pM[:, 0, 2 * P:3 * P], queryT[:], pm[:], start=True, stop=True).then_inc(w_pe, 1)
                pe.wait_ge(bdw_ready, b + 1)
                for c in range(CT):
                    last = mm(pM[:, c // 4, (c % 4) * P:(c % 4 + 1) * P], xnT[:, c * P:(c + 1) * P], bdw[:], start=True, stop=True)
                last.then_inc(attn_pe, 1)

            def jobs(base, w13, w2, ks, e, hid):
                wide = 2 * hid > 512
                for c in range(CT + 1):
                    if c < CT:
                        pe.wait_ge(hj_ready, base + c + 1)
                        if wide:
                            mm(pG[:, c % 2, 0:hid], xnT[:, c * P:(c + 1) * P], w13[:, 0:hid], start=True, stop=True)
                            mm(pU[:, c % 2, 0:hid], xnT[:, c * P:(c + 1) * P], w13[:, hid:2 * hid], start=True, stop=True
                               ).then_inc(gu_ready, 1)
                        else:
                            mm(pG[:, c % 2, 0:2 * hid], xnT[:, c * P:(c + 1) * P], w13, start=True, stop=True
                               ).then_inc(gu_ready, 1)
                    if c >= 1:
                        j = c - 1
                        pe.wait_ge(hj_ready, base + j + 1 + 2)
                        pe.wait_ge(y_used, base + j + 1)
                        for i, k in enumerate(ks):
                            last = pe.transpose(pT[0:k, j % 2, i * P:(i + 1) * P], hj[:, j % 2, i * P:i * P + k], ident[:])
                        last.then_inc(hT_pe, 1)
                        pe.wait_ge(hT_copied, base + j + 1)
                        for i, k in enumerate(ks):
                            last = mm(pT[:, j % 2, 3 * P:4 * P], hT[0:k, j % 2, i * P:(i + 1) * P], w2[0:k, i, :],
                                      start=(i == 0), stop=(i == len(ks) - 1))
                        last.then_inc(y_pe, 1)

            def experts(b, l):
                base = (2 * b + l) * JOBS
                if b == 0 and l == 0:
                    pe.wait_ge(scaled, 1)
                with pe.Fori(0, NE + l) as e:
                    if l == 0:
                        jobs(base + e * CT, w13a[:, bass.ds(e, 1), :].rearrange("p o h -> p (o h)"),
                             w2a[:, bass.ds(e, 1), :, :].rearrange("p o k d -> p (o k) d"), K0, e, H0)
                    else:
                        jobs(base + e * CT, w13b[:, bass.ds(e, 1), :].rearrange("p o h -> p (o h)"),
                             w2b[:, bass.ds(e, 1), :, :].rearrange("p o k d -> p (o k) d"), K1, e, H1)
                if l == 0:
                    jobs(base + NE * CT, w13s[:], w2s[:], K0S, None, S0)

            for b in range(NB):
                front(b, 0)
                mixer(b)
                experts(b, 0)
                front(b, 1)
                attn(b)
                experts(b, 1)

        @block.scalar
        def _(act):
            A = act.activation

            def front(b, l):
                i = 2 * b + l
                for m in range(2):
                    act.wait_ge(xnT_pe, 2 * i + m + 1)
                    A(xnT[:, m * 512:(m + 1) * 512], pM[:, m, :], ACT.Copy).then_inc(xnT_copied, 1)
                act.wait_ge(zl_ready, i + 1)
                A(el[:], zl[:], ACT.Exp).then_inc(el_ready, 1)
                if l == 1:
                    A(tsg[:], pM[:, 0, 0:128].rearrange("p (c e) -> p c e", e=16)[:, :, NE], ACT.Tanh, scale=0.5
                      ).then_inc(tsg_ready, 1)

            def mixer(b):
                for q in (2 * b, 2 * b + 1):
                    for m in range(4):
                        act.wait_ge(in_pe, 4 * q + m + 1)
                        if m < 2:
                            if m == 0:
                                act.wait_ge(conv_ready, 2 * q + 1)
                            A(xs[:, m, 3:3 + HALF], pM[:, m, :], ACT.Copy).then_inc(xs_copied, 1)
                        else:
                            A(th[:, m - 2, :], pM[:, m % 2, :], ACT.Tanh, scale=0.5).then_inc(th_ready, 1)
                    act.wait_ge(conv_ready, 2 * q + 2)
                    A(v[:], ca[:], ACT.Tanh).then_inc(thc_ready, 1)
                    act.wait_ge(dbl_pe, q + 1)
                    if q:
                        act.wait_ge(rows_stored, 16 * q)
                    A(dbl[:], pM[0:R + 2 * NS, 0, :], ACT.Copy).then_inc(dbl_copied, 1)
                    act.wait_ge(xc_ready, 2 * q + 2)
                    for k in range(DK):
                        act.wait_ge(dtr_pe, 2 * q + k + 1)
                        A(v[:, k, :], pM[:, 1 - k, :], ACT.Identity, bias=bdt[:, k:k + 1]).then_inc(v_ready, 1)
                    act.wait_ge(v_ready, 2 * q + 2)
                    A(ln[:], v[:], ACT.Abs).then_inc(chain, 1)
                    act.wait_ge(chain, 2 * q + 2)
                    A(ea[:], ln[:], ACT.Exp, scale=-1.0).then_inc(chain, 1)
                    act.wait_ge(chain, 2 * q + 3)
                    A(ln[:], ea[:], ACT.Ln, bias=1.0).then_inc(ln_ready, 1)
                    act.wait_ge(dt_ready, q + 1)
                    for n in range(NS):
                        N = q * NS + n
                        if N >= 2:
                            act.wait_ge(h_ready, 2 * (N - 1))
                        for k in range(DK):
                            A(dA[:, n % 2, k, :], dt[:, k, :], ACT.Exp, scale=am[:, k, n:n + 1]).then_inc(dA_ready, 1)
                        if q % 2 == 0 and n >= 1:
                            act.wait_ge(h_ready, 2 * N)
                            A(carry[:, :, n - 1], h[:, (n - 1) % 2, :, HALF - 1], ACT.Copy).then_inc(carried, 1)
                    if q % 2 == 0:
                        act.wait_ge(h_ready, 2 * NS * (q + 1))
                        A(carry[:, :, NS - 1], h[:, (NS - 1) % 2, :, HALF - 1], ACT.Copy).then_inc(carried, 1)

            def attn(b):
                act.wait_ge(pm_pe, b + 1)
                A(pm[:], pM[:, 0, P:2 * P], ACT.Copy).then_inc(pm_ready, 1)

            def jobs(base, ks, hid, uo):
                nk = len(ks)
                for c in range(CT + 1):
                    if c < CT:
                        act.wait_ge(gu_ready, base + c + 1)
                        act.wait_ge(a_ready, base + c + 1)
                        A(tj[:, c % 2, 0:hid], pG[:, c % 2, 0:hid], ACT.Tanh).then_inc(tanh_ready, 1)
                    if c >= 1:
                        j = c - 1
                        act.wait_ge(hT_pe, base + j + 1 + 2)
                        act.wait_ge(y_pe, base + j + 1)
                        A(hT[:, j % 2, 0:(nk - 1) * P], pT[:, j % 2, 0:(nk - 1) * P], ACT.Copy)
                        A(hT[0:ks[-1], j % 2, (nk - 1) * P:nk * P], pT[0:ks[-1], j % 2, (nk - 1) * P:nk * P], ACT.Copy
                          ).then_inc(hT_copied, 1)

            def experts(b, l):
                base = (2 * b + l) * JOBS
                with act.Fori(0, NE + l) as e:
                    jobs(base + e * CT, (K0, K1)[l], (H0, H1)[l], None)
                if l == 0:
                    jobs(base + NE * CT, K0S, S0, None)
                act.wait_ge(y_used, base + JOBS + 2)
                A(tg[:], moe[:], ACT.Tanh, scale=0.5).then_inc(tg_ready, 1)

            act.wait_ge(mixer_loaded, N_MIX)
            A(am[:], am[:], ACT.Exp).then_inc(chain, 1)
            for b in range(NB):
                front(b, 0)
                mixer(b)
                experts(b, 0)
                front(b, 1)
                attn(b)
                experts(b, 1)

        @block.vector
        def _(dve):
            V = dve
            cnt = [0]
            dchain = sem("dve_chain")

            def link(ins):
                cnt[0] += 1
                ins.then_inc(dchain, 1)
                dve.wait_ge(dchain, cnt[0])

            def setup():
                V.memset(pT[:], 0.0).then_inc(hj_ready, 2)
                V.memset(tj[:, 0, 0:8], 0.0).then_inc(y_used, 2)
                V.memset(tj[:, 0, 8:16], 0.0).then_inc(a_ready, 2)
                V.memset(tj[:, 0, 16:24], 0.0).then_inc(hT_pe, 2)
                V.memset(tj[:, 0, 24:32], 0.0).then_inc(y_pe, 2)
                dve.wait_ge(mixer_loaded, N_MIX)
                link(V.tensor_scalar(cw[:], cw[:], 0.5, None, ALU.mult))
                link(V.tensor_scalar(cb[:], cb[:], 0.5, None, ALU.mult))
                dve.wait_ge(chain, 1)
                link(V.tensor_scalar(am[:], am[:], -1.0, None, ALU.mult))
                link(V.memset(xs[:], 0.0))
                link(V.memset(bd[:], 0.0))
                link(V.memset(bdw[:], 0.0))
                V.memset(comb[:], 1.0).then_inc(dchain, 1)
                cnt[0] += 1

            def setup_experts():
                dve.wait_ge(loaded, N_EXP)
                V.tensor_scalar(w13a[:, :, 0:H0], w13a[:, :, 0:H0], 0.5, None, ALU.mult)
                V.tensor_scalar(w13s[:, 0:S0], w13s[:, 0:S0], 0.5, None, ALU.mult)
                V.tensor_scalar(w13b[:, :, 0:H1], w13b[:, :, 0:H1], 0.5, None, ALU.mult).then_inc(scaled, 1)

            def bc(ap, n):
                return ap.rearrange("p (c o) -> p c o", o=1).broadcast_to([P, CT, n])

            def front(b, l):
                i = 2 * b + l
                for c in range(CT):
                    last = V.bn_stats(stats[:, c, :], x[:, c, :])
                link(last)
                for c in range(CT):
                    last = V.bn_aggr(mv[:, c, :], stats[:, c, :])
                last.then_inc(stats_ready, 1)
                dve.wait_ge(rstd_ready, i + 1)
                dve.wait_ge(stats_ready, i + 1)
                for c in range(CT):
                    last = V.tensor_scalar(xn[:, c, :], x[:, c, :], mv[:, c, 0:1], rstd[:, c:c + 1], ALU.subtract, ALU.mult)
                last.then_inc(xn_ready, 1)
                dve.wait_ge(logits_pe, i + 1)
                lg = pM[:, 0, 0:128].rearrange("p (c e) -> p c e", e=16)
                link(V.tensor_reduce(mx[:], lg[:, :, 0:NE], op=ALU.max, axis=AX))
                V.tensor_tensor(zl[:], lg[:, :, 0:NE], bc(mx[:], NE), ALU.subtract).then_inc(zl_ready, 1)
                dve.wait_ge(el_ready, i + 1)
                link(V.tensor_reduce(se[:], el[:], op=ALU.add, axis=AX))
                link(V.reciprocal(se[:], se[:]))
                link(V.tensor_tensor(pr[:], el[:], bc(se[:], NE), ALU.mult))
                for c in range(CT):
                    last = V.max(top[:, c, :], pr[:, c, :])
                link(last)
                for c in range(CT):
                    last = V.max_index(idx[:, c, :], top[:, c, :], pr[:, c, :])
                link(last)
                link(V.tensor_copy(idf[:], idx[:, :, 0:2]))
                if l == 0:
                    wts = top
                else:
                    link(V.tensor_reduce(se[:], top[:, :, 0:2], op=ALU.add, axis=AX))
                    link(V.reciprocal(se[:], se[:]))
                    link(V.tensor_tensor(wk[:], top[:, :, 0:2], bc(se[:], 2), ALU.mult))
                    wts = wk
                io = iota8[:].rearrange("p (o e) -> p o e", o=1).broadcast_to([P, CT, NE])
                for k in range(2):
                    link(V.tensor_tensor(oh[:, k], io, idf[:, :, k:k + 1].broadcast_to([P, CT, NE]), ALU.is_equal))
                    link(V.tensor_tensor(oh[:, k], oh[:, k], wts[:, :, k:k + 1].broadcast_to([P, CT, NE]), ALU.mult))
                link(V.tensor_tensor(comb[:, :, 0:NE], oh[:, 0], oh[:, 1], ALU.add))
                if l == 1:
                    dve.wait_ge(tsg_ready, b + 1)
                    link(V.tensor_scalar(comb[:, :, NE], tsg[:], 0.5, 0.5, ALU.mult, ALU.add))
                else:
                    link(V.memset(comb[:, :, NE], 1.0))
                link(V.memset(moe[:], 0.0))

            def mixer(b):
                for q in (2 * b, 2 * b + 1):
                    hf = q % 2
                    if hf == 0:
                        V.memset(xs[:, :, 0:3], 0.0).then_inc(conv_ready, 1)
                    else:
                        V.tensor_copy(xs[:, :, 0:3], xs[:, :, HALF:HALF + 3]).then_inc(conv_ready, 1)
                    dve.wait_ge(xs_copied, 2 * q + 2)
                    dve.wait_ge(conv_ready, 2 * q + 1)
                    if q:
                        dve.wait_ge(thc_ready, q)
                    for k in range(DK):
                        link(V.tensor_scalar(ca[:, k, :], xs[:, k, 3:3 + HALF], cw[:, k, 3:4], cb[:, k:k + 1], ALU.mult, ALU.add))
                        for j in (2, 1, 0):
                            last = V.scalar_tensor_tensor(out=ca[:, k, :], in0=xs[:, k, j:j + HALF], scalar=cw[:, k, j:j + 1],
                                                          in1=ca[:, k, :], op0=ALU.mult, op1=ALU.add)
                            if j or k == 0:
                                link(last)
                    last.then_inc(conv_ready, 1)
                    for k in range(DK):
                        dve.wait_ge(th_ready, 2 * q + k + 1)
                        V.scalar_tensor_tensor(out=zs[:, k, :], in0=th[:, k, :], scalar=1.0, in1=pM[:, k, :],
                                               op0=ALU.add, op1=ALU.mult)
                    dve.wait_ge(thc_ready, q + 1)
                    dve.wait_ge(conv_ready, 2 * q + 2)
                    V.scalar_tensor_tensor(out=xc[:], in0=v[:], scalar=1.0, in1=ca[:], op0=ALU.add, op1=ALU.mult
                                           ).then_inc(xc_ready, 2)
                    dve.wait_ge(ln_ready, q + 1)
                    link(V.tensor_scalar(g[:], ea[:], 1.0, None, ALU.add))
                    link(V.scalar_tensor_tensor(out=g[:], in0=g[:], scalar=1.0, in1=ea[:], op0=ALU.subtract, op1=ALU.subtract))
                    link(V.tensor_tensor(g[:], ln[:], g[:], ALU.subtract))
                    V.scalar_tensor_tensor(out=dt[:], in0=v[:], scalar=0.0, in1=g[:], op0=ALU.max, op1=ALU.add
                                           ).then_inc(dt_ready, 1)
                    dve.wait_ge(dt_ready, q + 1)
                    dve.wait_ge(xc_ready, 2 * q + 2)
                    V.tensor_tensor(dtx[:], dt[:], xc[:], ALU.mult).then_inc(dtx_ready, 1)
                    for n in range(NS):
                        N = q * NS + n
                        r = n % 2
                        dve.wait_ge(dBx_ready, N + 1)
                        if N >= 2 and (q % 2 == 0 or n < 2):
                            dve.wait_ge(carried, min((q // 2) * NS + (n if q % 2 == 0 else NS) - 1, NS * (q // 2 + 1)) if q % 2 == 0 else NS * (q // 2 + 1))
                        for k in range(DK):
                            dve.wait_ge(dA_ready, 2 * N + k + 1)
                            V.tensor_tensor_scan(h[:, r, k, :], dA[:, r, k, :], dBx[:, r, k, :],
                                                 carry[:, k, n:n + 1] if hf else 0.0, ALU.mult, ALU.add).then_inc(h_ready, 1)
                        if n % GB == 0:
                            dve.wait_ge(bc_loaded[n // GB % 2], 32 * (((NS // GB) * q + n // GB) // 2 + 1))
                        dve.wait_ge(h_ready, 2 * N + 2)
                        crow = bcc[:, n // GB % 2, n % GB:n % GB + 1, :].broadcast_to([P, DK, HALF])
                        if n == 0:
                            V.tensor_tensor(y[:], h[:, r], crow, ALU.mult).then_inc(g_ready, 1)
                            dve.wait_ge(g_ready, N + 1)
                        else:
                            V.tensor_tensor(g[:], h[:, r], crow, ALU.mult).then_inc(g_ready, 1)
                            dve.wait_ge(g_ready, N + 1)
                            link(V.tensor_tensor(y[:], y[:], g[:], ALU.add))
                    for k in range(DK):
                        link(V.scalar_tensor_tensor(out=y[:, k, :], in0=xc[:, k, :], scalar=dpar[:, k:k + 1], in1=y[:, k, :],
                                                    op0=ALU.mult, op1=ALU.add))
                    V.scalar_tensor_tensor(out=y[:], in0=y[:], scalar=0.5, in1=zs[:], op0=ALU.mult, op1=ALU.mult
                                           ).then_inc(y2_ready, 1)
                    dve.wait_ge(out_pe, q + 1)
                    V.tensor_copy(s_sb[:, 4 * hf:4 * hf + 4, :], pM[:, 1, :].rearrange("p (c d) -> p c d", d=P)
                                  ).then_inc(s_copied, 1)

            def attn(b):
                dve.wait_ge(gram_pe, b + 1)
                for a in range(4):
                    r = slice(32 * a, 32 * a + 32)
                    last = V.tensor_copy(bd[r, r], pM[r, 0, r])
                last.then_inc(bd_ready, 1)
                dve.wait_ge(w_pe, b + 1)
                for a in range(4):
                    r = slice(32 * a, 32 * a + 32)
                    last = V.tensor_copy(bdw[r, r], pM[r, 0, 2 * P + 32 * a:2 * P + 32 * a + 32])
                last.then_inc(bdw_ready, 1)
                dve.wait_ge(attn_pe, b + 1)
                V.tensor_copy(s_sb[:], pM[:].rearrange("p m (c d) -> p (m c) d", d=P)).then_inc(s_copied, 1)

            def jobs(base, hid, ce):
                u = lambda c: pU[:, c % 2, 0:hid] if 2 * hid > 512 else pG[:, c % 2, hid:2 * hid]
                for c in range(CT + 1):
                    if c < CT:
                        dve.wait_ge(tanh_ready, base + c + 1)
                        V.scalar_tensor_tensor(out=aj[:, c % 2, 0:hid], in0=tj[:, c % 2, 0:hid], scalar=1.0,
                                               in1=pG[:, c % 2, 0:hid], op0=ALU.add, op1=ALU.mult).then_inc(a_ready, 1)
                        dve.wait_ge(a_ready, base + c + 1 + 2)
                        dve.wait_ge(hT_pe, base + c + 1)
                        V.tensor_tensor(hj[:, c % 2, 0:hid], aj[:, c % 2, 0:hid], u(c), ALU.mult).then_inc(hj_ready, 1)
                    if c >= 1:
                        j = c - 1
                        dve.wait_ge(y_pe, base + j + 1 + 2)
                        V.scalar_tensor_tensor(out=moe[:, j, :], in0=pT[:, j % 2, 3 * P:4 * P], scalar=ce(j), in1=moe[:, j, :],
                                               op0=ALU.mult, op1=ALU.add).then_inc(y_used, 1)

            def experts(b, l):
                base = (2 * b + l) * JOBS
                if b == 0 and l == 0:
                    setup_experts()
                with dve.Fori(0, NE + l) as e:
                    jobs(base + e * CT, (H0, H1)[l], lambda j: comb[:, j, bass.ds(e, 1)])
                if l == 0:
                    jobs(base + NE * CT, S0, lambda j: comb[:, j, NE:NE + 1])
                dve.wait_ge(tg_ready, 2 * b + l + 1)
                dve.wait_ge(s_copied, 3 * b + 2 + l)
                link(V.scalar_tensor_tensor(out=tg[:], in0=tg[:], scalar=1.0, in1=moe[:], op0=ALU.add, op1=ALU.mult))
                link(V.tensor_tensor(tg[:], tg[:], s_sb[:], ALU.mult))
                last = V.scalar_tensor_tensor(out=x[:], in0=tg[:], scalar=0.5, in1=x[:], op0=ALU.mult, op1=ALU.add)
                if l == 0:
                    link(last)
                else:
                    last.then_inc(x_out, 1)

            setup()
            for b in range(NB):
                dve.wait_ge(x_in, 16 * (b + 1))
                front(b, 0)
                mixer(b)
                experts(b, 0)
                front(b, 1)
                attn(b)
                experts(b, 1)


def kernel(**inputs):
    import numpy as np
    import concourse.bacc as bacc
    from concourse.bass_utils import run_bass_kernel_spmd

    def half(a):
        return np.ascontiguousarray(np.asarray(a).reshape(DK, P).T)

    nc = bacc.Bacc("TRN2", target_bir_lowering=False, num_devices=1)
    arrays = {n: np.ascontiguousarray(inputs[n]) for n in (
        "L0_attn_x", "L0_attn_W_in", "L0_attn_conv_w", "L0_attn_W_x", "L0_attn_W_dt", "L0_attn_A_log", "L0_attn_W_out",
        "L0_ffn_w1", "L0_ffn_w2", "L0_ffn_w3", "L0_ffn_sw1", "L0_ffn_sw2", "L0_ffn_sw3", "L1_ffn_w_gate", "L1_ffn_w_up",
        "L1_ffn_w_down", "L1_ffn_sw_gate", "L1_ffn_sw_up", "L1_ffn_sw_down")}
    arrays["conv_b"], arrays["b_dt"], arrays["D_param"] = (half(inputs["L0_attn_" + n]) for n in ("conv_b", "b_dt", "D_param"))
    arrays["gate0T"] = np.ascontiguousarray(np.asarray(inputs["L0_ffn_gate_w"]).T)
    arrays["gate1T"] = np.ascontiguousarray(
        np.concatenate([np.asarray(inputs["L1_ffn_gate_w"]), np.asarray(inputs["L1_ffn_shared_gate_w"])]).T)
    arrays["combi"] = np.ascontiguousarray(np.asarray(inputs["L1_attn_combiners"]).transpose(1, 0, 2).reshape(P, P))
    arrays["queryT"] = np.ascontiguousarray(np.asarray(inputs["L1_attn_queries"]).transpose(2, 0, 1).reshape(P, P))
    T = {n: nc.dram_tensor(f"in_{n}", a.shape, mybir.dt.from_np(a.dtype), kind="ExternalInput").ap() for n, a in arrays.items()}
    out = nc.dram_tensor("out_0", (NB, L, P), F32, kind="ExternalOutput").ap()
    program(nc, T, out)
    r = run_bass_kernel_spmd(nc, [{f"in_{n}": a for n, a in arrays.items()}], core_ids=[0])
    return r.results[0]["out_0"]
```

```python
from contextlib import ExitStack

import concourse.bass as bass
from concourse import mybir

F32 = mybir.dt.float32
U32 = mybir.dt.uint32
ALU = mybir.AluOpType
ACT = mybir.ActivationFunctionType
AX = mybir.AxisListType.X

P = 128
NB, L = 4, 1024
CT = L // P
HALF = 512
CH = NB * L // HALF
HT = HALF // P
NS = 16
DI = 256
DK = DI // P
R = 64
NE = 8
TOPK = 2
H0, S0, H1 = 352, 192, 176
HID = {(0, "routed"): H0, (0, "shared"): S0, (1, "routed"): H1, (1, "shared"): H1}
TILES = (TOPK * L + NE * (P - 1)) // P
YROWS = (TILES + CT) * P
GB = 2
NG = NS // GB
EPS = 1e-5
STEPS = CH * NS


def chunks(width):
    return [min(P, width - a) for a in range(0, width, P)]


def make_plan():
    extras = {}

    def at(step, *stage):
        extras.setdefault(step, []).append(stage)

    avail = {}

    def front(l, b, s, per_step):
        at(s, "norm", l, b)
        at(s + 1, "xn", l, b)
        at(s + 2, "xT", l, b, 0)
        at(s + 3, "xT", l, b, 1)
        at(s + 4, "logits", l, b)
        at(s + 5, "top", l, b)
        at(s + 6, "route", l, b)
        at(s + 7, "rank", l, b)
        at(s + 8, "slots", l, b)
        for i in range(TOPK * CT):
            at(s + 9 + i // per_step, "scatter", l, b, i)
        if l == 1:
            at(s + 2, "gram", b)
            at(s + 3, "pm", b)
            at(s + 4, "wm", b)
            at(s + 5, "attn", b, 0)
            at(s + 6, "attn", b, 1)
        avail[l, b, "shared"] = s + 4
        avail[l, b, "routed"] = s + 10 + TOPK * CT // per_step

    def mixer_front(q, s):
        at(s, "xs", q, 0)
        at(s + 1, "xs", q, 1)
        at(s + 2, "conv", q, 0)
        at(s + 3, "conv", q, 1)
        at(s + 3, "thc", q)
        at(s + 4, "xc", q)
        at(s + 5, "dbl", q)
        at(s + 6, "ct", q)
        at(s + 6, "dtr", q, 0)
        at(s + 7, "dtr", q, 1)
        at(s + 7, "soft", q)
        at(s + 8, "ln", q)
        at(s + 10, "dt", q)

    for q in range(1, CH):
        mixer_front(q, 16 * (q - 1) + 3)
    for q in range(CH):
        at(16 * q + 2, "z", q, 0)
        at(16 * q + 4, "z", q, 1)
        at(16 * q + 5, "zsilu", q)
    for b in range(1, NB):
        at(max(0, 32 * (b - 1) - 6), "xload", b)
        front(0, b, 32 * (b - 1) + 1, 3)
    avail[0, 0, "shared"] = avail[0, 0, "routed"] = 0
    for b in range(NB):
        s = 32 * (b + 1)
        at(s, "fetch", 0, b)
        for part in range(3):
            at(s + 1 + part, "combine", 0, b, part)
        front(1, b, s + (16 if b < NB - 2 else 4), 3 if b < NB - 1 else 8)

    order = [(l, b, kind, i) for l in range(2) for b in range(NB)
             for kind, count in (("shared", CT), ("routed", TILES)) for i in range(count)]
    todo = {0: [j for j in order if j[0] == 0], 1: [j for j in order if j[0] == 1]}
    lanes = {0: [], 1: []}
    starts = {}
    last = {}
    step = 0
    while todo[0] or todo[1]:
        for r in range(2):
            for lane in (0, 1):
                if r == 1 and (lane == 1 or step % 2 or step >= STEPS):
                    continue
                pick = todo[0] if lane == 0 and todo[0] else todo[1]
                if lane == 0 and not todo[0] and step < 60:
                    continue
                if pick and avail[pick[0][:3]] <= step:
                    if r == 1 and pick is todo[1]:
                        continue
                    job = pick.pop(0)
                    starts.setdefault((step, r), {})[lane] = len(lanes[lane])
                    lanes[lane].append(job)
                    last[job[:2]] = step
        step += 1
    end = step
    for b in range(NB):
        s0 = 32 * (b + 1) - 8
        assert s0 > last[0, b] + 1
        for i in range(TOPK * CT):
            at(s0 + i // 3, "gather", 0, b, i)
        s1 = max(last[1, b] + 3, 32 * min(b + 3, NB) + 5)
        if s1 > STEPS - 24:
            s1 = max(s1, STEPS + 8 + 4 * b)
        per = 3 if s1 < STEPS else 8
        at(s1, "fetch", 1, b)
        for i in range(TOPK * CT):
            at(s1 + i // per, "gather", 1, b, i)
        for part in range(3):
            at(s1 + 15 // per + 1 + part, "combine", 1, b, part)

    plan = [("xload", 0), ("norm", 0, 0), ("xn", 0, 0), ("xT", 0, 0, 0), ("xT", 0, 0, 1), ("xs", 0, 0), ("xs", 0, 1),
            ("logits", 0, 0), ("conv", 0, 0), ("conv", 0, 1), ("top", 0, 0), ("thc", 0), ("xc", 0), ("dbl", 0), ("ct", 0), ("dtr", 0, 0), ("dtr", 0, 1),
            ("route", 0, 0), ("rank", 0, 0), ("soft", 0), ("ln", 0), ("slots", 0, 0), ("dt", 0)]
    plan += [("scatter", 0, 0, i) for i in range(TOPK * CT)]
    plan += [("decay", 0)]
    running, waiting = [None, None], [None, None]
    fetched, tiled = [0, 0], [0, 0]

    def slot(lane, new, step):
        cur, out = running[lane], waiting[lane]
        if new is None and cur is None and out is None:
            return
        if cur is not None:
            plan.append(("gate", lane, cur))
        if new is not None:
            while fetched[lane] < min(new + 5, len(lanes[lane])) and avail[lanes[lane][fetched[lane]][:3]] <= step:
                plan.append(("tile", lane, fetched[lane]))
                fetched[lane] += 1
            first = None
            if tiled[lane] <= new:
                tiled[lane] = new + 1
                first = new
            ahead = None
            if fetched[lane] > new + 1:
                tiled[lane] = new + 2
                ahead = new + 1
            plan.append(("up", lane, new, first, ahead))
        if cur is not None or out is not None:
            plan.append(("flip", lane, cur, out))
        running[lane], waiting[lane] = new, cur

    for step in range(max(end + 3, max(extras) + 1)):
        q, n = divmod(step, NS)
        new = starts.get((step, 0), {})
        if step < STEPS:
            plan.append(("scan", step))
        slot(0, new.get(0), step)
        slot(1, new.get(1), step)
        if 0 < step <= STEPS:
            plan.append(("sum", step - 1))
            if n == 0:
                plan.append(("accT", q - 1))
                if (step, 1) in starts:
                    slot(0, starts.pop((step, 1))[0], step)
                plan.append(("y", q - 1))
        if step < STEPS:
            plan.append(("hflip", step))
        if step and n == 0 and step <= STEPS:
            plan.append(("mix_out", q - 1))
        if (step, 1) in starts:
            slot(0, starts[step, 1][0], step)
        plan += extras.get(step, [])
    return plan, lanes


def program(nc, T, out):
    plan, lanes = make_plan()

    use, flip_use = {}, {}

    def takes(*key):
        use[key] = len(use) + 1

    fronts, combos = [], []
    for it in plan:
        if it[0] in ("xT", "logits", "rank", "xs", "dbl", "ct", "dtr", "z", "mix_out", "gram", "pm", "wm", "attn"):
            takes(*it)
        elif it[0] == "flip":
            takes(*it)
            if it[2] is not None:
                flip_use[it[1], it[2]] = len(use)
        if it[0] == "norm":
            fronts.append(it[1:])
        if it[0] == "combine" and it[3] == 0:
            combos.append(it[1:3])
    front_no = {f: n + 1 for n, f in enumerate(fronts)}
    combo_no = {f: n for n, f in enumerate(combos)}
    gram_no = {f[1]: n + 1 for n, f in enumerate(f for f in fronts if f[0] == 1)}
    routed_before = {i: [sum(j[2] == "routed" for j in lanes[i][:k]) for k in range(len(lanes[i]) + 1)] for i in lanes}
    ends = {(i, j[:2]): k + 1 for i in lanes for k, j in enumerate(lanes[i])}
    mix_stores = [it for it in plan if it[0] in ("mix_out", "attn")]
    mix_no = {it: n for n, it in enumerate(mix_stores)}
    tile_ahead = {it[2]: routed_before[0][it[4]] + 1 for it in plan
                  if it[0] == "up" and it[1] == 0 and it[4] is not None and lanes[0][it[4]][2] == "routed"}
    wide_before = [sum(2 * HID[j[0], j[2]] > 512 for j in lanes[0][:k]) for k in range(len(lanes[0]) + 1)]
    carries = [sum((m // NS) % 2 == 0 for m in range(N + 1)) for N in range(STEPS)]

    with ExitStack() as ctx:
        def sb(name, shape, dt=F32):
            return ctx.enter_context(nc.sbuf_tensor(name, shape, dt))

        def ps(name, shape):
            return ctx.enter_context(nc.psum_tensor(name, shape, F32))

        def sem(name):
            return ctx.enter_context(nc.semaphore(name))

        w13a = sb("w13a", [P, NE, 2 * H0])
        w2a = sb("w2a", [P, NE, 3, P])
        w13s = sb("w13s", [P, 2 * S0])
        w2s = sb("w2s", [P, 2, P])
        w13b = sb("w13b", [P, NE + 1, 2 * H1])
        w2b = sb("w2b", [P, NE + 1, 2, P])
        w_in = sb("w_in", [P, 2 * DI])
        w_x = sb("w_x", [P, DK, R + 2 * NS])
        w_dt = sb("w_dt", [R, DI])
        w_out = sb("w_out", [P, DK, P])
        cw = sb("cw", [P, DK, 4])
        cb = sb("cb", [P, DK])
        bdt = sb("bdt", [P, DK])
        am = sb("am", [P, DK, NS])
        dpar = sb("dpar", [P, DK])
        gate = [sb("gate0", [P, NE]), sb("gate1", [P, NE + 1])]
        combi = sb("combi", [P, P])
        queryT = sb("queryT", [P, P])
        NCONST = 3 * P + NE + NE * CT + TILES + NE
        const = sb("const", [P, NCONST])
        ident, before, ones = (const[:, k * P:(k + 1) * P] for k in range(3))
        iota8 = const[:, 3 * P:3 * P + NE]
        steps128 = const[:, 3 * P + NE:3 * P + NE + NE * CT]
        tile_no = const[:, 3 * P + NE + NE * CT:3 * P + NE + NE * CT + TILES]
        mhalf = const[:, NCONST - NE:NCONST]

        x = sb("x", [P, CT, P])
        xn = sb("xn", [P, CT, P])
        xnT = [[sb("xnT0", [P, L]), sb("xnT1", [P, L])], [sb("x1T", [P, L])] * 2]
        stats = sb("stats", [P, CT, 6])
        mv = sb("mv", [P, CT, 2])
        vpe = sb("vpe", [P, CT])
        rstd = sb("rstd", [P, CT])
        lg = sb("lg", [P, CT, NE + 1])
        mx = sb("mx", [P, CT])
        zl = sb("zl", [P, CT, NE])
        el = sb("el", [P, CT, NE])
        se = sb("se", [P, CT])
        pr = sb("pr", [P, CT, NE])
        top = sb("top", [P, CT, 8])
        idx = sb("idx", [P, CT, 8], U32)
        idf = sb("idf", [P, CT, 2])
        oh = sb("oh", [P, TOPK, CT, NE])
        picked = sb("picked", [P, CT, NE])
        rk = sb("rk", [P, CT + 1, NE])
        over = sb("over", [P, NE, CT])
        nt = sb("nt", [P, NE])
        incl = sb("incl", [P, NE])
        excl = sb("excl", [P, NE])
        slotf = sb("slotf", [P, CT, TOPK])
        cmp = sb("cmp", [P, TILES, NE])
        tef = sb("tef", [P, TILES])
        wts = [[sb(f"wts{l}{b}", [P, CT, TOPK]) for b in range(NB)] for l in range(2)]
        slots = [[sb(f"slots{l}{b}", [P, CT, TOPK], U32) for b in range(NB)] for l in range(2)]
        expert = [[sb(f"expert{l}{b}", [P, TILES], U32) for b in range(NB)] for l in range(2)]
        sg = sb("sg", [P, NB, CT])
        bd = sb("bd", [P, P])
        pm = sb("pm", [P, P])
        bdw = sb("bdw", [P, P])
        gy = sb("gy", [P, TOPK, CT, P])
        so = sb("so", [P, CT, P])
        sr = sb("sr", [P, CT, P])
        xr = sb("xr", [P, CT, P])
        s_st = sb("s_st", [P, HT, P])

        xs = sb("xs", [P, DK, HALF + 3])
        ca = sb("ca", [P, DK, HALF])
        v = sb("v", [P, DK, HALF])
        dbl = sb("dbl", [R + NS, HALF])
        zs = sb("zs", [P, DK, HALF])
        xc = [sb(f"xc{i}", [P, DK, HALF]) for i in range(2)]
        dt = [sb(f"dt{i}", [P, DK, HALF]) for i in range(2)]
        dtx = [sb(f"dtx{i}", [P, DK, HALF]) for i in range(2)]
        ct = sb("ct", [P, 2, HT, NS])
        bcb = sb("bcb", [P, 2, GB, HALF])
        dBx = sb("dBx", [P, 2, DK, HALF])
        h = sb("h", [P, 2, DK, HALF])
        carry = sb("carry", [P, DK, NS])
        acc = sb("acc", [P, HT, DI])
        y = sb("y", [P, DK, HALF])
        LW, YR = [H0, H1], 4
        xg = [sb(f"xg{i}", [P, 4, P]) for i in range(2)]
        xgT = [sb(f"xgT{i}", [P, P]) for i in range(2)]
        tj = [sb(f"tj{i}", [P, LW[i]]) for i in range(2)]
        hj = [sb(f"hj{i}", [P, 2, LW[i]]) for i in range(2)]
        hT = [sb(f"hT{i}", [P, (3 - i) * P]) for i in range(2)]
        yj = [sb(f"yj{i}", [P, YR, P]) for i in range(2)]

        def dram(name, shape):
            return nc.dram_tensor(name, shape, F32, kind="Internal").ap()

        b_rows = [dram(f"b_rows{q}", (NS, HALF)) for q in range(CH)]
        rows_in = [[dram(f"rows_in{l}{i}", (TILES * P, P)) for i in range(2)] for l in range(2)]
        rows_out = [[dram(f"rows_out{l}{b}", (YROWS, P)) for b in range(NB)] for l in range(2)]
        mixed = [[dram(f"mixed{l}{b}", (L, P)) for b in range(NB)] for l in range(2)]
        mid = [dram(f"mid{b}", (L, P)) for b in range(NB)]

        pA = ps("pA", [P, DK, HALF])
        pH = ps("pH", [P, 2, 512])
        pG = ps("pG", [P, 512])
        pU = ps("pU", [P, 512])
        p1 = ps("p1", [P, 512])
        pM = ps("pM", [P, 512])
        bank, tile_bank = [pG, p1], [pU, p1]
        TA = 2 * H1
        YA = 3 * P

        mix_loaded, exp_loaded, zeroed, zero_tile = sem("mix_loaded"), sem("exp_loaded"), sem("zeroed"), sem("zero_tile")
        psum_cleared, scaled, decay_exp, prepared = sem("psum_cleared"), sem("scaled"), sem("decay_exp"), sem("prepared")
        bank_full, bank_read = sem("bank_full"), sem("bank_read")
        gate_full = sem("gate_full")
        x_in, stats_ready, ve_ready, rstd_ready, xn_ready = (
            sem("x_in"), sem("stats_ready"), sem("ve_ready"), sem("rstd_ready"), sem("xn_ready"))
        zl_ready, el_ready, picked_ready, slots_ready, sg_ready = (
            sem("zl_ready"), sem("el_ready"), sem("picked_ready"), sem("slots_ready"), sem("sg_ready"))
        scattered = [[sem(f"scattered{l}{i}") for i in range(2)] for l in range(2)]
        halo_ready, conv_ready, thc_ready, xc_ready = sem("halo_ready"), sem("conv_ready"), sem("thc_ready"), sem("xc_ready")
        rows_stored, act_chain, ln_ready, dt_ready, dtx_ready = (
            sem("rows_stored"), sem("act_chain"), sem("ln_ready"), sem("dt_ready"), sem("dtx_ready"))
        b_loaded = [sem("b_loaded0"), sem("b_loaded1")]
        y_ready, accT_full = sem("y_ready"), sem("accT_full")
        decay_ready, dBx_ready, h_ready, hflip_full, sum_done, carried = (
            sem("decay_ready"), sem("dBx_ready"), sem("h_ready"), sem("hflip_full"), sem("sum_done"), sem("carried"))
        mixed_stored, gathered, fetched, combined, mid_stored, out_stored = (
            sem("mixed_stored"), [sem("gathered0"), sem("gathered1")], sem("fetched"), sem("combined"), sem("mid_stored"),
            sem("out_stored"))
        sum_ready, tg_ready = sem("sum_ready"), sem("tg_ready")
        dve_chain = sem("dve_chain")
        tile_in = [[sem(f"tile_in{i}{s}") for s in range(4)] for i in range(2)]
        tile_full, tile_copied = [sem(f"tile_full{i}") for i in range(2)], [sem(f"tile_copied{i}") for i in range(2)]
        gu_full, tanh_ready = [sem(f"gu_full{i}") for i in range(2)], [sem(f"tanh_ready{i}") for i in range(2)]
        a_ready, hj_ready = [sem(f"a_ready{i}") for i in range(2)], [sem(f"hj_ready{i}") for i in range(2)]
        out_rows = [[sem(f"out_rows{i}{s}") for s in range(YR)] for i in range(2)]

        block = ctx.enter_context(nc.Block())

        mix_loads = [
            (const[:], T["const"]),
            (w_in[:], T["L0_attn_W_in"]),
            (w_x[:], T["L0_attn_W_x"].rearrange("(k p) n -> p k n", p=P)),
            (w_dt[:], T["L0_attn_W_dt"]),
            (w_out[:], T["L0_attn_W_out"].rearrange("(k p) n -> p k n", p=P)),
            (cw[:], T["L0_attn_conv_w"].rearrange("(k p) j -> p k j", p=P)),
            (cb[:], T["conv_b"]), (bdt[:], T["b_dt"]), (dpar[:], T["D_param"]),
            (am[:], T["L0_attn_A_log"].rearrange("(k p) n -> p k n", p=P)),
            (gate[0][:], T["gate0T"]), (gate[1][:], T["gate1T"]),
            (combi[:], T["combi"]), (queryT[:], T["queryT"]),
        ]
        w1, w3, w2 = T["L0_ffn_w1"], T["L0_ffn_w3"], T["L0_ffn_w2"]
        v1, v3, v2 = T["L1_ffn_w_gate"], T["L1_ffn_w_up"], T["L1_ffn_w_down"]
        exp_loads = [
            (w13s[:, 0:S0], T["L0_ffn_sw1"]), (w13s[:, S0:2 * S0], T["L0_ffn_sw3"]),
            (w2s[:, 0, :], T["L0_ffn_sw2"][0:128, :]), (w2s[0:64, 1, :], T["L0_ffn_sw2"][128:192, :]),
            (w13a[:, :, 0:H0], w1.rearrange("e d h -> d e h")),
            (w13a[:, :, H0:2 * H0], w3.rearrange("e d h -> d e h")),
            (w2a[:, :, 0, :], w2[:, 0:128, :].rearrange("e h d -> h e d")),
            (w2a[:, :, 1, :], w2[:, 128:256, :].rearrange("e h d -> h e d")),
            (w2a[0:96, :, 2, :], w2[:, 256:352, :].rearrange("e h d -> h e d")),
            (w13b[:, 0:NE, 0:H1], v1.rearrange("e d h -> d e h")),
            (w13b[:, 0:NE, H1:2 * H1], v3.rearrange("e d h -> d e h")),
            (w13b[:, NE, 0:H1], T["L1_ffn_sw_gate"]), (w13b[:, NE, H1:2 * H1], T["L1_ffn_sw_up"]),
            (w2b[:, 0:NE, 0, :], v2[:, 0:128, :].rearrange("e h d -> h e d")),
            (w2b[0:48, 0:NE, 1, :], v2[:, 128:176, :].rearrange("e h d -> h e d")),
            (w2b[:, NE, 0, :], T["L1_ffn_sw_down"][0:128, :]), (w2b[0:48, NE, 1, :], T["L1_ffn_sw_down"][128:176, :]),
        ]
        by_tile = "(c p) d -> p c d"

        @block.sync
        def _(sp):
            for kind, *a in plan:
                if kind == "xload":
                    b, = a
                    if b:
                        sp.wait_ge(xn_ready, front_no[0, b - 1])
                    sp.dma_start(x[:], T["L0_attn_x"][b].rearrange(by_tile, p=P)).then_inc(x_in, 16)
                    if b == 0:
                        for dst, src in mix_loads:
                            sp.dma_start(dst, src).then_inc(mix_loaded, 16)
                        sp.wait_ge(zero_tile, 1)
                        for l in range(2):
                            for i in range(2):
                                rows = rows_in[l][i].rearrange(by_tile, p=P)
                                for c in range(0, TILES, CT):
                                    n = min(CT, TILES - c)
                                    sp.dma_start(rows[:, c:c + n, :], gy[:, 0, 0:n, :]).then_inc(zeroed, 16)
                            if l == 0:
                                for dst, src in exp_loads:
                                    sp.dma_start(dst, src).then_inc(exp_loaded, 16)
                elif kind == "dbl":
                    q, = a
                    sp.wait_ge(bank_read, use["dbl", q])
                    sp.dma_start(b_rows[q], dbl[R:R + NS, :]).then_inc(rows_stored, 16)
                elif kind == "tile":
                    i, k = a
                    l, b, what, t = lanes[i][k]
                    if what == "routed":
                        m = routed_before[i][k]
                        if m >= 4:
                            sp.wait_ge(tile_full[i], m - 3)
                        sp.wait_ge(scattered[l][b % 2], 16 * TOPK * CT * (b // 2 + 1))
                        sp.dma_start(xg[i][:, m % 4, :], rows_in[l][b % 2][t * P:(t + 1) * P, :]).then_inc(tile_in[i][m % 4], 16)
                elif kind == "flip" and a[2] is not None:
                    i, _, k = a
                    l, b, what, t = lanes[i][k]
                    sp.wait_ge(bank_read, use[(kind, *a)])
                    r = t if what == "routed" else TILES + t
                    sp.dma_start(rows_out[l][b][r * P:(r + 1) * P, :], yj[i][:, k % YR, :]).then_inc(out_rows[i][k % YR], 16)
                elif kind in ("mix_out", "attn"):
                    it = (kind, *a)
                    l, b, m = (0, a[0] // 2, a[0] % 2) if kind == "mix_out" else (1, a[0], a[1])
                    sp.wait_ge(bank_read, use[it])
                    sp.dma_start(mixed[l][b][m * HALF:(m + 1) * HALF, :].rearrange(by_tile, p=P), s_st[:]
                                 ).then_inc(mixed_stored, 16)
                elif kind == "fetch":
                    l, b = a
                    n = combo_no[l, b]
                    if n:
                        pl, pb = combos[n - 1]
                        sp.wait_ge(combined, n)
                        if pl == 0:
                            sp.wait_ge(xn_ready, front_no[1, pb])
                            sp.wait_ge(mid_stored, 16 * (pb + 1))
                        else:
                            sp.wait_ge(out_stored, 16 * (pb + 1))
                    for i in range(2):
                        if (i, (l, b)) in ends:
                            for r in range(min(YR, ends[i, (l, b)])):
                                sp.wait_ge(out_rows[i][r], 16 * ((ends[i, (l, b)] - r + YR - 1) // YR))
                    sp.dma_start(so[:], rows_out[l][b][TILES * P:, :].rearrange(by_tile, p=P)).then_inc(fetched, 16)
                    src = T["L0_attn_x"][b] if l == 0 else mid[b]
                    sp.dma_start(xr[:], src.rearrange(by_tile, p=P)).then_inc(fetched, 16)
                    final = mix_no[("mix_out", 2 * b + 1) if l == 0 else ("attn", b, 1)]
                    sp.wait_ge(mixed_stored, 16 * (final + 1))
                    sp.dma_start(sr[:], mixed[l][b].rearrange(by_tile, p=P)).then_inc(fetched, 16)
                elif kind == "combine" and a[2] == 2:
                    l, b = a[:2]
                    sp.wait_ge(combined, combo_no[l, b] + 1)
                    if l == 0:
                        sp.dma_start(mid[b].rearrange(by_tile, p=P), xr[:]).then_inc(mid_stored, 16)
                    else:
                        sp.dma_start(out[b].rearrange(by_tile, p=P), xr[:]).then_inc(out_stored, 16)
            sp.wait_ge(out_stored, 16 * NB)

        @block.gpsimd
        def _(pool):
            for kind, *a in plan:
                if kind == "norm":
                    F = front_no[tuple(a)]
                    if F == 1:
                        pool.wait_ge(mix_loaded, 16 * len(mix_loads))
                    pool.wait_ge(stats_ready, F)
                    if F > 1:
                        pool.wait_ge(xn_ready, F - 1)
                    pool.tensor_scalar(vpe[:], mv[:, :, 1], EPS, None, ALU.add).then_inc(ve_ready, 1)
                    pool.wait_ge(ve_ready, F)
                    pool.tensor_tensor(rstd[:], vpe[:], mhalf, ALU.pow).then_inc(rstd_ready, 1)
                elif kind == "scatter":
                    l, b, i = a
                    c, k = divmod(i, TOPK)
                    if i == 0:
                        pool.wait_ge(slots_ready, front_no[l, b])
                        if b < 2:
                            pool.wait_ge(zeroed, 16 * 4 * ((TILES + CT - 1) // CT))
                        else:
                            for lane in range(2):
                                if (lane, (l, b - 2)) in ends:
                                    pool.wait_ge(tile_full[lane], routed_before[lane][ends[lane, (l, b - 2)]])
                    pool.indirect_dma_start(rows_in[l][b % 2], bass.IndirectOffsetOnAxis(ap=slots[l][b][:, c, k:k + 1], axis=0),
                                            xn[:, c, :], None).then_inc(scattered[l][b % 2], 16)
                elif kind == "gather":
                    l, b, i = a
                    c, k = divmod(i, TOPK)
                    n = combo_no[l, b]
                    if i == 0:
                        for lane in range(2):
                            if (lane, (l, b)) in ends:
                                for r in range(min(YR, ends[lane, (l, b)])):
                                    pool.wait_ge(out_rows[lane][r], 16 * ((ends[lane, (l, b)] - r + YR - 1) // YR))
                        if n:
                            pool.wait_ge(combined, n)
                    pool.indirect_dma_start(gy[:, k, c, :], None, rows_out[l][b],
                                            bass.IndirectOffsetOnAxis(ap=slots[l][b][:, c, k:k + 1], axis=0)
                                            ).then_inc(gathered[n % 2], 16)
                elif kind in ("decay", "scan"):
                    N = 0 if kind == "decay" else a[0] + 1
                    if N == STEPS:
                        continue
                    q, n = divmod(N, NS)
                    G = N // GB
                    if n == 0:
                        pool.wait_ge(dtx_ready, q + 1)
                    if N % GB == 0:
                        pool.wait_ge(b_loaded[G % 2], 16 * (G // 2 + 1))
                    if N >= 2:
                        pool.wait_ge(h_ready, 2 * (N - 1))
                    row = bcb[:, G % 2, N % GB:N % GB + 1, :].broadcast_to([P, DK, HALF])
                    pool.tensor_tensor(dBx[:, N % 2], dtx[q % 2][:], row, ALU.mult).then_inc(dBx_ready, 1)

        @block.tensor
        def _(pe):
            mm = pe.matmul

            def take(*key):
                if use[key] > 1:
                    pe.wait_ge(bank_read, use[key] - 1)

            expert_reg = [[pe.alloc_register(f"expert{i}{j}") for j in range(4)] for i in range(2)]
            expert_of = [[None] * 4, [None] * 4]

            for kind, *a in plan:
                if kind == "xload" and a[0] == 0:
                    pe.wait_ge(mix_loaded, 16 * len(mix_loads))
                    pe.wait_ge(prepared, 1)
                elif kind == "xT":
                    l, b, m = a
                    pe.wait_ge(xn_ready, front_no[l, b])
                    take(*("xT", *a))
                    for c in range(4):
                        last = pe.transpose(pM[:, c * P:(c + 1) * P], xn[:, 4 * m + c, :], ident)
                    last.then_inc(bank_full, 1)
                elif kind == "logits":
                    l, b = a
                    take("logits", l, b)
                    for c in range(CT):
                        last = mm(pM[:, 16 * c:16 * c + NE + l], xnT[l][b % 2][:, c * P:(c + 1) * P], gate[l][:], start=True, stop=True)
                    last.then_inc(bank_full, 1)
                elif kind == "rank":
                    l, b = a
                    pe.wait_ge(picked_ready, front_no[l, b])
                    take("rank", l, b)
                    flat = picked[:].rearrange("p c e -> p (c e)")
                    mm(pM[:, 0:CT * NE], before, flat, start=True, stop=False)
                    for c in range(CT - 1):
                        mm(pM[:, (c + 1) * NE:CT * NE].rearrange("p (c e) -> p c e", e=NE), ones,
                           picked[:, c:c + 1, :].broadcast_to([P, CT - 1 - c, NE]), start=False, stop=(c == CT - 2))
                    for c in range(CT):
                        last = mm(pM[:, CT * NE:(CT + 1) * NE], ones, picked[:, c, :], start=(c == 0), stop=(c == CT - 1))
                    last.then_inc(bank_full, 1)
                elif kind == "gram":
                    take("gram", a[0])
                    for c in range(CT):
                        last = mm(pM[:, 0:P], xn[:, c, :], xn[:, c, :], start=(c == 0), stop=(c == CT - 1))
                    last.then_inc(bank_full, 1)
                elif kind == "pm":
                    take("pm", a[0])
                    mm(pM[:, 0:P], bd[:], combi[:], start=True, stop=True).then_inc(bank_full, 1)
                elif kind == "wm":
                    take("wm", a[0])
                    mm(pM[:, 0:P], queryT[:], pm[:], start=True, stop=True).then_inc(bank_full, 1)
                elif kind == "attn":
                    b, m = a
                    take("attn", b, m)
                    for c in range(4):
                        last = mm(pM[:, c * P:(c + 1) * P], xnT[1][0][:, (4 * m + c) * P:(4 * m + c + 1) * P], bdw[:], start=True, stop=True)
                    last.then_inc(bank_full, 1)
                elif kind in ("xs", "z"):
                    q, k = a
                    take(kind, q, k)
                    w = w_in[:, ((kind == "z") * DK + k) * P:((kind == "z") * DK + k + 1) * P]
                    mm(pM[:], w, xnT[0][q // 2 % 2][:, q % 2 * HALF:(q % 2 + 1) * HALF], start=True, stop=True).then_inc(bank_full, 1)
                elif kind == "dbl":
                    q, = a
                    pe.wait_ge(xc_ready, q + 1)
                    take("dbl", q)
                    for k in range(DK):
                        last = mm(pM[0:R + NS, :], w_x[:, k, 0:R + NS], xc[q % 2][:, k, :], start=(k == 0), stop=(k == DK - 1))
                    last.then_inc(bank_full, 1)
                elif kind == "ct":
                    q, = a
                    take("ct", q)
                    for c in range(HT):
                        for k in range(DK):
                            last = mm(pM[:, c * NS:(c + 1) * NS], xc[q % 2][:, k, c * P:(c + 1) * P], w_x[:, k, R + NS:],
                                      start=(k == 0), stop=(k == DK - 1))
                    last.then_inc(bank_full, 1)
                elif kind == "dtr":
                    q, k = a
                    if k == 0:
                        pe.wait_ge(bank_read, use["dbl", q])
                    take("dtr", q, k)
                    mm(pM[:], w_dt[:, k * P:(k + 1) * P], dbl[0:R, :], start=True, stop=True).then_inc(bank_full, 1)
                elif kind == "hflip":
                    N, = a
                    q, n = divmod(N, NS)
                    pe.wait_ge(h_ready, 2 * (N + 1))
                    if n == 0 and q:
                        pe.wait_ge(y_ready, q)
                    for half in range(2):
                        if N:
                            pe.wait_ge(sum_done, 2 * (N - 1) + half + 1)
                        for c in range(2):
                            for k in range(DK):
                                t = 2 * half + c
                                last = pe.transpose(pH[:, half, c * DI + k * P:c * DI + (k + 1) * P], h[:, N % 2, k, t * P:(t + 1) * P], ident)
                        last.then_inc(hflip_full, 1)
                elif kind == "accT":
                    q, = a
                    pe.wait_ge(sum_done, 2 * NS * (q + 1))
                    for k in range(DK):
                        for c in range(HT):
                            last = pe.transpose(pH[:, k, c * P:(c + 1) * P], acc[:, c, k * P:(k + 1) * P], ident)
                    last.then_inc(accT_full, 1)
                elif kind == "mix_out":
                    q, = a
                    pe.wait_ge(y_ready, q + 1)
                    take("mix_out", q)
                    for c in range(HT):
                        for k in range(DK):
                            last = mm(pM[:, c * P:(c + 1) * P], y[:, k, c * P:(c + 1) * P], w_out[:, k, :],
                                      start=(k == 0), stop=(k == DK - 1))
                    last.then_inc(bank_full, 1)
                elif kind == "up":
                    i, k, first, ahead = a
                    if k == 0:
                        pe.wait_ge(scaled, 1)
                    else:
                        pe.wait_ge(hj_ready[i], k)

                    def transpose_tile(j):
                        l, b, what, t = lanes[i][j]
                        m = routed_before[i][j]
                        pe.wait_ge(tile_in[i][m % 4], 16 * (m // 4 + 1))
                        pe.transpose(tile_bank[i][:, TA:TA + P], xg[i][:, m % 4, :], ident).then_inc(tile_full[i], 1)
                        pe.wait_ge(slots_ready, front_no[l, b])
                        pe.reg_load(expert_reg[i][j % 4], expert[l][b][0:1, t:t + 1])
                        expert_of[i][j % 4] = pe.snap(expert_reg[i][j % 4], min_val=0, max_val=NE - 1)

                    l, b, what, t = lanes[i][k]
                    hid = HID[l, what]
                    if first is not None and what == "routed":
                        transpose_tile(first)
                    if what == "routed":
                        pe.wait_ge(tile_copied[i], routed_before[i][k] + 1)
                        tok = xgT[i][:]
                        e = expert_of[i][k % 4]
                        w = (w13a, w13b)[l][:, bass.ds(e, 1), :].rearrange("p o h -> p (o h)")
                    else:
                        tok = xnT[l][b % 2][:, t * P:(t + 1) * P]
                        w = w13s[:] if l == 0 else w13b[:, NE, :]
                    if 2 * hid > 512:
                        mm(pG[:, 0:hid], tok, w[:, 0:hid], start=True, stop=True).then_inc(gate_full, 1)
                        mm(pU[:, 0:hid], tok, w[:, hid:2 * hid], start=True, stop=True).then_inc(gu_full[i], 1)
                    else:
                        mm(bank[i][:, 0:2 * hid], tok, w, start=True, stop=True).then_inc(gu_full[i], 1)
                    if ahead is not None and lanes[i][ahead][2] == "routed":
                        transpose_tile(ahead)
                elif kind == "flip":
                    i, k, before_k = a
                    if k is not None:
                        pe.wait_ge(hj_ready[i], k + 1)
                    take(*("flip", *a))
                    if k is not None:
                        for m, w in enumerate(chunks(HID[lanes[i][k][0], lanes[i][k][2]])):
                            last = pe.transpose(pM[0:w, m * P:(m + 1) * P], hj[i][:, k % 2, m * P:m * P + w], ident)
                    if before_k is not None:
                        l, b, what, t = lanes[i][before_k]
                        ks = chunks(HID[l, what])
                        if what == "routed":
                            e = expert_of[i][before_k % 4]
                            w = (w2a, w2b)[l][:, bass.ds(e, 1), :, :].rearrange("p o k d -> p (o k) d")
                        else:
                            w = w2s[:] if l == 0 else w2b[:, NE, :, :]
                        for m, wd in enumerate(ks):
                            last = mm(pM[:, YA:YA + P], hT[i][0:wd, m * P:(m + 1) * P], w[0:wd, m, :],
                                      start=(m == 0), stop=(m == len(ks) - 1))
                    last.then_inc(bank_full, 1)

        @block.scalar
        def _(act):
            A = act.activation

            def decay(N):
                q, n = divmod(N, NS)
                if n == 0:
                    act.wait_ge(dt_ready, q + 1)
                for k in range(DK):
                    if N:
                        act.wait_ge(h_ready, 2 * (N - 1) + k + 1)
                    A(pA[:, k, :], dt[q % 2][:, k, :], ACT.Exp, scale=am[:, k, n:n + 1]).then_inc(decay_ready, 1)

            def b_group(G):
                q, g = divmod(G, NG)
                if g == 0:
                    act.wait_ge(rows_stored, 16 * (q + 1))
                if G >= 2:
                    act.wait_ge(dBx_ready, GB * (G - 1))
                src = b_rows[q][g * GB:(g + 1) * GB, :].rearrange("(o n) t -> o n t", o=1)
                act.dma_start(bcb[:, G % 2, :, :], src.broadcast_to([P, GB, HALF])).then_inc(b_loaded[G % 2], 16)

            for kind, *a in plan:
                if kind == "xload" and a[0] == 0:
                    act.wait_ge(mix_loaded, 16 * len(mix_loads))
                    A(am[:], am[:], ACT.Exp).then_inc(decay_exp, 1)
                    act.wait_ge(prepared, 1)
                elif kind == "xT":
                    l, b, m = a
                    act.wait_ge(bank_full, use["xT", l, b, m])
                    A(xnT[l][b % 2][:, m * 512:(m + 1) * 512], pM[:], ACT.Copy).then_inc(bank_read, 1)
                elif kind == "logits":
                    l, b = a
                    act.wait_ge(bank_full, use["logits", l, b])
                    if front_no[l, b] > 1:
                        act.wait_ge(zl_ready, front_no[l, b] - 1)
                    A(lg[:, :, 0:NE + l], pM[:, 0:16 * CT].rearrange("p (c e) -> p c e", e=16)[:, :, 0:NE + l], ACT.Copy
                      ).then_inc(bank_read, 1)
                elif kind == "rank":
                    l, b = a
                    act.wait_ge(bank_full, use["rank", l, b])
                    A(rk[:].rearrange("p c e -> p (c e)"), pM[:, 0:(CT + 1) * NE], ACT.Copy).then_inc(bank_read, 1)
                elif kind == "gram":
                    b, = a
                    act.wait_ge(bank_full, use["gram", b])
                    for c in range(4):
                        r = slice(32 * c, 32 * c + 32)
                        last = A(bd[r, r], pM[r, r], ACT.Copy)
                    last.then_inc(bank_read, 1)
                elif kind == "top":
                    l, b = a
                    F = front_no[l, b]
                    act.wait_ge(zl_ready, F)
                    A(el[:], zl[:], ACT.Exp).then_inc(el_ready, 1)
                    if l == 1:
                        A(sg[:, b, :], lg[:, :, NE], ACT.Tanh, scale=0.5).then_inc(sg_ready, 1)
                elif kind == "pm":
                    b, = a
                    act.wait_ge(bank_full, use["pm", b])
                    A(pm[:], pM[:, 0:P], ACT.Copy).then_inc(bank_read, 1)
                elif kind == "wm":
                    b, = a
                    act.wait_ge(bank_full, use["wm", b])
                    for c in range(4):
                        r = slice(32 * c, 32 * c + 32)
                        last = A(bdw[r, r], pM[r, r], ACT.Copy)
                    last.then_inc(bank_read, 1)
                elif kind in ("attn", "mix_out"):
                    it = (kind, *a)
                    act.wait_ge(bank_full, use[it])
                    if mix_no[it]:
                        act.wait_ge(mixed_stored, 16 * mix_no[it])
                    A(s_st[:].rearrange("p c d -> p (c d)"), pM[:], ACT.Copy).then_inc(bank_read, 1)
                elif kind == "xs":
                    q, k = a
                    act.wait_ge(halo_ready, q + 1)
                    act.wait_ge(bank_full, use["xs", q, k])
                    A(xs[:, k, 3:3 + HALF], pM[:], ACT.Copy).then_inc(bank_read, 1)
                elif kind == "thc":
                    q, = a
                    act.wait_ge(conv_ready, 2 * (q + 1))
                    if q:
                        act.wait_ge(dt_ready, q)
                    A(v[:], ca[:], ACT.Tanh).then_inc(thc_ready, 1)
                elif kind == "dbl":
                    q, = a
                    act.wait_ge(bank_full, use["dbl", q])
                    if q:
                        act.wait_ge(rows_stored, 16 * q)
                    A(dbl[:], pM[0:R + NS, :], ACT.Copy).then_inc(bank_read, 1)
                elif kind == "ct":
                    q, = a
                    act.wait_ge(bank_full, use["ct", q])
                    A(ct[:, q % 2, :, :].rearrange("p c n -> p (c n)"), pM[:, 0:HT * NS], ACT.Copy).then_inc(bank_read, 1)
                elif kind == "dtr":
                    q, k = a
                    if k == 0:
                        act.wait_ge(xc_ready, q + 1)
                    act.wait_ge(bank_full, use["dtr", q, k])
                    A(v[:, k, :], pM[:], ACT.Identity, bias=bdt[:, k:k + 1]).then_inc(bank_read, 1)
                elif kind == "soft":
                    q, = a
                    act.wait_ge(bank_read, use["dtr", q, 1])
                    A(ca[:], v[:], ACT.Abs).then_inc(act_chain, 1)
                    act.wait_ge(act_chain, 2 * q + 1)
                    A(ca[:], ca[:], ACT.Exp, scale=-1.0).then_inc(act_chain, 1)
                elif kind == "ln":
                    q, = a
                    act.wait_ge(act_chain, 2 * q + 2)
                    A(dt[q % 2][:], ca[:], ACT.Ln, bias=1.0).then_inc(ln_ready, 1)
                elif kind == "z":
                    q, k = a
                    act.wait_ge(bank_full, use["z", q, k])
                    if q:
                        act.wait_ge(y_ready, q)
                    A(zs[:, k, :], pM[:], ACT.Tanh, scale=0.5)
                    A(y[:, k, :], pM[:], ACT.Copy).then_inc(bank_read, 1)
                elif kind == "decay":
                    b_group(0)
                    b_group(1)
                    act.wait_ge(prepared, 2)
                    decay(0)
                elif kind == "scan":
                    N, = a
                    q, n = divmod(N, NS)
                    if N + 1 < STEPS:
                        decay(N + 1)
                    if N % GB == GB - 1 and N // GB + 2 < CH * NG:
                        b_group(N // GB + 2)
                    if q % 2 == 0:
                        act.wait_ge(h_ready, 2 * N + 2)
                        A(carry[:, :, n], h[:, N % 2, :, HALF - 1], ACT.Copy).then_inc(carried, 1)
                elif kind == "up":
                    i, k, first, ahead = a
                    l, b, what, t = lanes[i][k]
                    hid = HID[l, what]

                    def copy_tile(j):
                        act.wait_ge(tile_full[i], routed_before[i][j] + 1)
                        A(xgT[i][:], tile_bank[i][:, TA:TA + P], ACT.Copy).then_inc(tile_copied[i], 1)

                    if first is not None and what == "routed":
                        copy_tile(first)
                    if 2 * hid > 512:
                        act.wait_ge(gate_full, wide_before[k] + 1)
                        A(tj[i][:, 0:hid], bank[i][:, 0:hid], ACT.Tanh).then_inc(tanh_ready[i], 1)
                    act.wait_ge(gu_full[i], k + 1)
                    if ahead is not None and lanes[i][ahead][2] == "routed":
                        copy_tile(ahead)
                    if 2 * hid <= 512:
                        A(tj[i][:, 0:hid], bank[i][:, 0:hid], ACT.Tanh).then_inc(tanh_ready[i], 1)
                elif kind == "flip":
                    i, k, before_k = a
                    act.wait_ge(bank_full, use[("flip", *a)])
                    if before_k is not None:
                        if before_k >= YR:
                            act.wait_ge(out_rows[i][before_k % YR], 16 * (before_k // YR))
                        last = A(yj[i][:, before_k % YR, :], pM[:, YA:YA + P], ACT.Copy)
                    if k is not None:
                        w = P * len(chunks(HID[lanes[i][k][0], lanes[i][k][2]]))
                        last = A(hT[i][:, 0:w], pM[:, 0:w], ACT.Copy)
                    last.then_inc(bank_read, 1)
                elif kind == "combine" and a[2] == 1:
                    l, b = a[:2]
                    n = combo_no[l, b]
                    act.wait_ge(sum_ready, n + 1)
                    A(gy[:, 1], gy[:, 0], ACT.Tanh, scale=0.5).then_inc(tg_ready, 1)

        @block.vector
        def _(dve):
            cnt = [0]

            def link(ins):
                cnt[0] += 1
                ins.then_inc(dve_chain, 1)
                dve.wait_ge(dve_chain, cnt[0])

            def per_token(ap, n):
                return ap.rearrange("p (c o) -> p c o", o=1).broadcast_to([P, CT, n])

            dve.memset(gy[:, 0], 0.0).then_inc(zero_tile, 1)
            for t in (pA, pH, pG, pU, p1, pM):
                dve.memset(t[:], 0.0)
            dve.memset(xs[:], 0.0)
            dve.memset(bd[:], 0.0)
            dve.memset(bdw[:], 0.0).then_inc(prepared, 1)
            dve.wait_ge(mix_loaded, 16 * len(mix_loads))
            dve.tensor_scalar(cw[:], cw[:], 0.5, None, ALU.mult)
            dve.tensor_scalar(cb[:], cb[:], 0.5, None, ALU.mult)
            dve.wait_ge(decay_exp, 1)
            dve.tensor_scalar(am[:], am[:], -1.0, None, ALU.mult).then_inc(prepared, 1)
            dve.wait_ge(prepared, 2)

            for kind, *a in plan:
                if kind == "norm":
                    l, b = a
                    F = front_no[l, b]
                    src = x if l == 0 else xr
                    if l == 0:
                        dve.wait_ge(x_in, 16 * (b + 1))
                    for c in range(CT):
                        last = dve.bn_stats(stats[:, c, :], src[:, c, :])
                    link(last)
                    for c in range(CT):
                        last = dve.bn_aggr(mv[:, c, :], stats[:, c, :])
                    last.then_inc(stats_ready, 1)
                elif kind == "xn":
                    l, b = a
                    F = front_no[l, b]
                    src = x if l == 0 else xr
                    dve.wait_ge(stats_ready, F)
                    dve.wait_ge(rstd_ready, F)
                    if F > 1:
                        pl, pb = fronts[F - 2]
                        dve.wait_ge(scattered[pl][pb % 2], 16 * TOPK * CT * (pb // 2 + 1))
                    for c in range(CT):
                        last = dve.tensor_scalar(xn[:, c, :], src[:, c, :], mv[:, c, 0:1], rstd[:, c:c + 1], ALU.subtract, ALU.mult)
                    last.then_inc(xn_ready, 1)
                elif kind == "top":
                    l, b = a
                    dve.wait_ge(bank_read, use["logits", l, b])
                    link(dve.tensor_reduce(mx[:], lg[:, :, 0:NE], op=ALU.max, axis=AX))
                    dve.tensor_tensor(zl[:], lg[:, :, 0:NE], per_token(mx[:], NE), ALU.subtract).then_inc(zl_ready, 1)
                elif kind == "route":
                    l, b = a
                    F = front_no[l, b]
                    dve.wait_ge(el_ready, F)
                    link(dve.tensor_reduce(se[:], el[:], op=ALU.add, axis=AX))
                    link(dve.reciprocal(se[:], se[:]))
                    link(dve.tensor_tensor(pr[:], el[:], per_token(se[:], NE), ALU.mult))
                    for c in range(CT):
                        last = dve.max(top[:, c, :], pr[:, c, :])
                    link(last)
                    for c in range(CT):
                        last = dve.max_index(idx[:, c, :], top[:, c, :], pr[:, c, :])
                    link(last)
                    link(dve.tensor_copy(idf[:], idx[:, :, 0:TOPK]))
                    io = iota8.rearrange("p (o e) -> p o e", o=1).broadcast_to([P, CT, NE])
                    for k in range(TOPK):
                        last = dve.tensor_tensor(oh[:, k], io, idf[:, :, k:k + 1].broadcast_to([P, CT, NE]), ALU.is_equal)
                    link(last)
                    dve.tensor_tensor(picked[:], oh[:, 0], oh[:, 1], ALU.add).then_inc(picked_ready, 1)
                    if l == 0:
                        link(dve.tensor_copy(wts[l][b][:], top[:, :, 0:TOPK]))
                    else:
                        link(dve.tensor_reduce(se[:], top[:, :, 0:TOPK], op=ALU.add, axis=AX))
                        link(dve.reciprocal(se[:], se[:]))
                        link(dve.tensor_tensor(wts[l][b][:], top[:, :, 0:TOPK], per_token(se[:], TOPK), ALU.mult))
                        dve.wait_ge(sg_ready, b + 1)
                        link(dve.tensor_scalar(sg[:, b, :], sg[:, b, :], 0.5, 0.5, ALU.mult, ALU.add))
                elif kind == "slots":
                    l, b = a
                    dve.wait_ge(bank_read, use["rank", l, b])
                    link(dve.tensor_tensor(over[:], rk[:, CT, :].rearrange("p (e o) -> p e o", o=1).broadcast_to([P, NE, CT]),
                                           steps128.rearrange("p (e m) -> p e m", m=CT), ALU.is_gt))
                    link(dve.tensor_reduce(nt[:], over[:], op=ALU.add, axis=AX))
                    link(dve.tensor_tensor_scan(incl[:], ones[:, 0:NE], nt[:], 0.0, ALU.mult, ALU.add))
                    link(dve.tensor_tensor(excl[:], incl[:], nt[:], ALU.subtract))
                    link(dve.scalar_tensor_tensor(out=rk[:, 0:CT, :], in0=excl[:].rearrange("p (o e) -> p o e", o=1).broadcast_to([P, CT, NE]),
                                                  scalar=float(P), in1=rk[:, 0:CT, :], op0=ALU.mult, op1=ALU.add))
                    for k in range(TOPK):
                        link(dve.tensor_tensor(oh[:, k], oh[:, k], rk[:, 0:CT, :], ALU.mult))
                        last = dve.tensor_reduce(slotf[:, :, k], oh[:, k], op=ALU.add, axis=AX)
                    link(last)
                    link(dve.tensor_copy(slots[l][b][:], slotf[:]))
                    link(dve.tensor_tensor(cmp[:], tile_no.rearrange("p (j o) -> p j o", o=1).broadcast_to([P, TILES, NE]),
                                           incl[:].rearrange("p (o e) -> p o e", o=1).broadcast_to([P, TILES, NE]), ALU.is_ge))
                    link(dve.tensor_reduce(tef[:], cmp[:], op=ALU.add, axis=AX))
                    dve.tensor_scalar(expert[l][b][:], tef[:], float(NE - 1), None, ALU.min).then_inc(slots_ready, 1)
                elif kind == "xs":
                    q, k = a
                    if k == 0:
                        if q % 2 == 0:
                            dve.memset(xs[:, :, 0:3], 0.0).then_inc(halo_ready, 1)
                        else:
                            dve.tensor_copy(xs[:, :, 0:3], xs[:, :, HALF:HALF + 3]).then_inc(halo_ready, 1)
                elif kind == "conv":
                    q, k = a
                    dve.wait_ge(bank_read, use["xs", q, 1])
                    dve.wait_ge(halo_ready, q + 1)
                    link(dve.tensor_scalar(ca[:, k, :], xs[:, k, 3:3 + HALF], cw[:, k, 3:4], cb[:, k:k + 1], ALU.mult, ALU.add))
                    for j in (2, 1, 0):
                        last = dve.scalar_tensor_tensor(out=ca[:, k, :], in0=xs[:, k, j:j + HALF], scalar=cw[:, k, j:j + 1],
                                                        in1=ca[:, k, :], op0=ALU.mult, op1=ALU.add)
                        if j:
                            link(last)
                    last.then_inc(conv_ready, 1)
                elif kind == "xc":
                    q, = a
                    dve.wait_ge(thc_ready, q + 1)
                    dve.wait_ge(conv_ready, 2 * q + 2)
                    dve.scalar_tensor_tensor(out=xc[q % 2][:], in0=v[:], scalar=1.0, in1=ca[:], op0=ALU.add, op1=ALU.mult
                                             ).then_inc(xc_ready, 1)
                elif kind == "dt":
                    q, = a
                    g = xs[:, :, 0:HALF]
                    dve.wait_ge(ln_ready, q + 1)
                    link(dve.tensor_scalar(g, ca[:], 1.0, None, ALU.add))
                    link(dve.scalar_tensor_tensor(out=g, in0=g, scalar=1.0, in1=ca[:], op0=ALU.subtract, op1=ALU.subtract))
                    link(dve.tensor_tensor(g, dt[q % 2][:], g, ALU.subtract))
                    dve.scalar_tensor_tensor(out=dt[q % 2][:], in0=v[:], scalar=0.0, in1=g, op0=ALU.max, op1=ALU.add
                                             ).then_inc(dt_ready, 1)
                    dve.wait_ge(dt_ready, q + 1)
                    dve.wait_ge(xc_ready, q + 1)
                    dve.tensor_tensor(dtx[q % 2][:], dt[q % 2][:], xc[q % 2][:], ALU.mult).then_inc(dtx_ready, 1)
                elif kind == "zsilu":
                    q, = a
                    dve.wait_ge(bank_read, use["z", q, 1])
                    link(dve.scalar_tensor_tensor(out=zs[:], in0=zs[:], scalar=1.0, in1=y[:], op0=ALU.add, op1=ALU.mult))
                elif kind == "scan":
                    N, = a
                    q, n = divmod(N, NS)
                    dve.wait_ge(dBx_ready, N + 1)
                    if N >= 2:
                        dve.wait_ge(hflip_full, 2 * (N - 1))
                        dve.wait_ge(carried, carries[N - 2])
                    if q % 2:
                        dve.wait_ge(carried, q // 2 * NS + n + 1)
                    for k in range(DK):
                        dve.wait_ge(decay_ready, 2 * N + k + 1)
                        dve.tensor_tensor_scan(h[:, N % 2, k, :], pA[:, k, :], dBx[:, N % 2, k, :],
                                               carry[:, k, n:n + 1] if q % 2 else 0.0, ALU.mult, ALU.add).then_inc(h_ready, 1)
                elif kind == "sum":
                    N, = a
                    q, n = divmod(N, NS)
                    if n == 0:
                        if q:
                            dve.wait_ge(accT_full, q)
                        dve.wait_ge(bank_read, use["ct", q])
                    for half in range(2):
                        dve.wait_ge(hflip_full, 2 * N + half + 1)
                        if n:
                            dve.wait_ge(sum_done, 2 * (N - 1) + half + 1)
                        for c in range(2):
                            t = 2 * half + c
                            src = pH[:, half, c * DI:(c + 1) * DI]
                            cn = ct[:, q % 2, t, n:n + 1]
                            if n == 0:
                                last = dve.tensor_scalar(acc[:, t, :], src, cn, None, ALU.mult)
                            else:
                                last = dve.scalar_tensor_tensor(out=acc[:, t, :], in0=src, scalar=cn, in1=acc[:, t, :],
                                                                op0=ALU.mult, op1=ALU.add)
                        last.then_inc(sum_done, 1)
                elif kind == "y":
                    q, = a
                    dve.wait_ge(accT_full, q + 1)
                    for k in range(DK):
                        last = dve.scalar_tensor_tensor(out=y[:, k, :], in0=xc[q % 2][:, k, :], scalar=dpar[:, k:k + 1], in1=pH[:, k, :],
                                                        op0=ALU.mult, op1=ALU.add)
                    link(last)
                    dve.scalar_tensor_tensor(out=y[:], in0=y[:], scalar=0.5, in1=zs[:], op0=ALU.mult, op1=ALU.mult).then_inc(y_ready, 1)
                elif kind == "tile":
                    if a[0] == 0 and a[1] == 0:
                        dve.wait_ge(exp_loaded, 16 * len(exp_loads))
                        dve.tensor_scalar(w13a[:, :, 0:H0], w13a[:, :, 0:H0], 0.5, None, ALU.mult)
                        dve.tensor_scalar(w13s[:, 0:S0], w13s[:, 0:S0], 0.5, None, ALU.mult)
                        dve.tensor_scalar(w13b[:, :, 0:H1], w13b[:, :, 0:H1], 0.5, None, ALU.mult).then_inc(scaled, 1)
                elif kind == "gate":
                    i, k = a
                    l, b, what, t = lanes[i][k]
                    hid = HID[l, what]
                    up = pU[:, 0:hid] if 2 * hid > 512 else bank[i][:, hid:2 * hid]
                    dve.wait_ge(tanh_ready[i], k + 1)
                    if k >= 2:
                        dve.wait_ge(bank_full, flip_use[i, k - 2])
                    dve.scalar_tensor_tensor(out=hj[i][:, k % 2, 0:hid], in0=tj[i][:, 0:hid], scalar=1.0, in1=bank[i][:, 0:hid],
                                             op0=ALU.add, op1=ALU.mult).then_inc(a_ready[i], 1)
                    dve.wait_ge(a_ready[i], k + 1)
                    if 2 * hid > 512:
                        dve.wait_ge(gu_full[i], k + 1)
                        if k in tile_ahead:
                            dve.wait_ge(tile_copied[i], tile_ahead[k])
                    dve.tensor_tensor(hj[i][:, k % 2, 0:hid], hj[i][:, k % 2, 0:hid], up, ALU.mult).then_inc(hj_ready[i], 1)
                elif kind == "combine":
                    l, b, part = a
                    n = combo_no[l, b]
                    if part == 0:
                        dve.wait_ge(gathered[n % 2], 16 * TOPK * CT * (n // 2 + 1))
                        for k in range(TOPK):
                            last = dve.tensor_tensor(gy[:, k], gy[:, k], wts[l][b][:, :, k:k + 1].broadcast_to([P, CT, P]), ALU.mult)
                        link(last)
                        link(dve.tensor_tensor(gy[:, 0], gy[:, 0], gy[:, 1], ALU.add))
                    elif part == 1:
                        dve.wait_ge(fetched, 48 * (n + 1))
                        if l == 1:
                            link(dve.tensor_tensor(so[:], so[:], per_token(sg[:, b, :], P), ALU.mult))
                        dve.tensor_tensor(gy[:, 0], gy[:, 0], so[:], ALU.add).then_inc(sum_ready, 1)
                    else:
                        dve.wait_ge(tg_ready, n + 1)
                        link(dve.scalar_tensor_tensor(out=gy[:, 0], in0=gy[:, 1], scalar=1.0, in1=gy[:, 0], op0=ALU.add, op1=ALU.mult))
                        link(dve.tensor_tensor(gy[:, 0], gy[:, 0], sr[:], ALU.mult))
                        dve.scalar_tensor_tensor(out=xr[:], in0=gy[:, 0], scalar=0.5, in1=xr[:], op0=ALU.mult, op1=ALU.add
                                                 ).then_inc(combined, 1)
                        dve.wait_ge(combined, n + 1)


def kernel(**inputs):
    import numpy as np
    import concourse.bacc as bacc
    from concourse.bass_utils import run_bass_kernel_spmd

    def half(a):
        return np.ascontiguousarray(np.asarray(a).reshape(DK, P).T)

    nc = bacc.Bacc("TRN2", target_bir_lowering=False, num_devices=1)
    arrays = {n: np.ascontiguousarray(inputs[n]) for n in (
        "L0_attn_x", "L0_attn_W_in", "L0_attn_conv_w", "L0_attn_W_x", "L0_attn_W_dt", "L0_attn_A_log", "L0_attn_W_out",
        "L0_ffn_w1", "L0_ffn_w2", "L0_ffn_w3", "L0_ffn_sw1", "L0_ffn_sw2", "L0_ffn_sw3", "L1_ffn_w_gate", "L1_ffn_w_up",
        "L1_ffn_w_down", "L1_ffn_sw_gate", "L1_ffn_sw_up", "L1_ffn_sw_down")}
    arrays["conv_b"], arrays["b_dt"], arrays["D_param"] = (half(inputs["L0_attn_" + n]) for n in ("conv_b", "b_dt", "D_param"))
    arrays["gate0T"] = np.ascontiguousarray(np.asarray(inputs["L0_ffn_gate_w"]).T)
    arrays["gate1T"] = np.ascontiguousarray(
        np.concatenate([np.asarray(inputs["L1_ffn_gate_w"]), np.asarray(inputs["L1_ffn_shared_gate_w"])]).T)
    arrays["combi"] = np.ascontiguousarray(np.asarray(inputs["L1_attn_combiners"]).transpose(1, 0, 2).reshape(P, P))
    arrays["queryT"] = np.ascontiguousarray(np.asarray(inputs["L1_attn_queries"]).transpose(2, 0, 1).reshape(P, P))
    row = np.ones((P, 1), np.float32)
    arrays["const"] = np.ascontiguousarray(np.concatenate([
        np.eye(P), np.triu(np.ones((P, P)), 1), np.ones((P, P)), row * np.arange(NE), row * np.tile(P * np.arange(CT), NE),
        row * np.arange(TILES), row * np.full(NE, -0.5)], axis=1).astype(np.float32))
    T = {n: nc.dram_tensor(f"in_{n}", a.shape, mybir.dt.from_np(a.dtype), kind="ExternalInput").ap() for n, a in arrays.items()}
    out = nc.dram_tensor("out_0", (NB, L, P), F32, kind="ExternalOutput").ap()
    program(nc, T, out)
    r = run_bass_kernel_spmd(nc, [{f"in_{n}": a for n, a in arrays.items()}], core_ids=[0])
    return r.results[0]["out_0"]
```

```python
from contextlib import ExitStack

import concourse.bass as bass
from concourse import mybir

F32 = mybir.dt.float32
U32 = mybir.dt.uint32
ALU = mybir.AluOpType
ACT = mybir.ActivationFunctionType
AX = mybir.AxisListType.X

P = 128
NB, L = 4, 1024
CT = L // P
HALF = 512
CH = NB * L // HALF
HT = HALF // P
NS = 16
DI = 256
DK = DI // P
R = 64
NE = 8
TOPK = 2
H0, S0, H1 = 352, 192, 176
HID = {(0, "routed"): H0, (0, "shared"): S0, (1, "routed"): H1, (1, "shared"): H1}
TILES = (TOPK * L + NE * (P - 1)) // P
YROWS = (TILES + CT) * P
GB = 2
NG = NS // GB
EPS = 1e-5
STEPS = CH * NS
WITH_SECOND = "a scan b sum c hflip".split()
WITH_ONE = "a scan b sum hflip".split()
AFTER_SCANS = "a A b B".split()
XS_AT, Z_AT, FRONT0_AT, FRONT1_AT = 2, 12, 1, 18
GATHER2_AT, COMBINE2_AT = 19, 22


def second_job(step):
    return step % (2 if step < 24 else 4) == 0


def chunks(width):
    return [min(P, width - a) for a in range(0, width, P)]


def pieces(l, b):
    return [(0, CT)] if (l, b) != (1, NB - 1) else [(0, CT // 2 + 1), (CT // 2 + 1, CT)]


def on_pool(l, b):
    return (l, b) in ((0, 0), (0, 1), (0, 2), (1, 0))


def make_plan():
    extras = {}

    def at(step, *stage):
        extras.setdefault(step, []).append(stage)

    avail = {}

    def front(l, b, s, per_step):
        at(s, "norm", l, b)
        at(s + 1, "xn", l, b)
        at(s + 2, "xT", l, b, 0)
        at(s + 3, "xT", l, b, 1)
        at(s + 4, "logits", l, b)
        at(s + 5, "top", l, b)
        at(s + 6, "route", l, b)
        at(s + 7, "rank", l, b)
        at(s + 8, "slots", l, b)
        for i in range(TOPK * CT):
            at(s + 9 + i // per_step, "scatter", l, b, i)
        if l == 1:
            at(s + 2, "gram", b)
            at(s + 3, "pm", b)
            at(s + 4, "wm", b)
            at(s + 5, "attn", b, 0)
            at(s + 6, "attn", b, 1)
        avail[l, b, "shared"] = s + 4
        avail[l, b, "routed"] = s + 10 + TOPK * CT // per_step

    def mixer_front(q, s):
        at(s, "xs", q, 0)
        at(s + 1, "xs", q, 1)
        at(s + 2, "conv", q, 0)
        at(s + 3, "conv", q, 1)
        at(s + 3, "thc", q)
        at(s + 4, "xc", q)
        at(s + 5, "dbl", q)
        at(s + 6, "ct", q)
        at(s + 6, "dtr", q, 0)
        at(s + 7, "dtr", q, 1)
        at(s + 7, "soft", q)
        at(s + 9, "ln", q)
        at(s + 10, "dt", q)

    for q in range(1, CH):
        mixer_front(q, 16 * (q - 1) + XS_AT)
    for q in range(CH):
        at(16 * q + Z_AT, "z", q, 0)
        at(16 * q + Z_AT + 2, "z", q, 1)
        at(16 * q + Z_AT + 3, "zsilu", q)
    for b in range(1, NB):
        at(max(0, 32 * (b - 1) - 6), "xload", b)
        front(0, b, 32 * (b - 1) + (10 if b == 1 else FRONT0_AT), 3)
    for s, kind in enumerate(("logits", "top", "route", "rank", "slots")):
        at(s, kind, 0, 0)
    for i in range(TOPK * CT):
        at(5 + i // 4, "scatter", 0, 0, i)
    avail[0, 0, "shared"], avail[0, 0, "routed"] = 1, 10
    for b in range(NB):
        s = 32 * (b + 1)
        at(s - 1, "fetch", 0, b)
        at(s, "fetch_mixed", 0, b)
        for part in range(6):
            when = (-1, 0, 1, 2, 3, 3)[part] if b < NB - 1 else part // 2 - 1
            at(s + when, "combine", 0, b, part, 0)
        front(1, b, s + (FRONT1_AT if b < NB - 2 else 3 if b < NB - 1 else 2), 3 if b < NB - 1 else 8)

    order = [(l, b, kind, i) for l in range(2) for b in range(NB)
             for kind, count in (("shared", CT), ("routed", TILES)) for i in range(count)]
    todo = {0: [j for j in order if j[0] == 0], 1: [j for j in order if j[0] == 1]}
    lanes = {0: [], 1: []}
    starts = {}
    last = {}
    step = 0
    while todo[0] or todo[1]:
        for r in range(2):
            for lane in (0, 1):
                if r == 1 and (lane == 1 or not second_job(step) or step >= STEPS):
                    continue
                pick = todo[0] if lane == 0 and todo[0] else todo[1]
                if lane == 1 and step % 4 == 2 and todo[0]:
                    continue
                if pick and avail[pick[0][:3]] <= step:
                    if r == 1 and pick is todo[1]:
                        continue
                    job = pick.pop(0)
                    starts.setdefault((step, r), {})[lane] = len(lanes[lane])
                    lanes[lane].append(job)
                    last[job[:2]] = step
        step += 1
    end = step
    for b in range(NB):
        s0 = 32 * (b + 1) - 5
        assert s0 > last[0, b] + 2
        for i in range(TOPK * CT):
            at(s0 + i // 4 - (b > 0), "gather", 0, b, i)
        s1 = last[1, b] + 3
        if s1 < STEPS + 5 and (s1 + 16) % 32 < 21:
            s1 += 21 - (s1 + 16) % 32
        per, start = (3, s1 + 6) if s1 < STEPS else (8, s1 + 2)
        if b == 1:
            start = STEPS + 13
        elif b == NB - 2:
            s1, start = STEPS + GATHER2_AT, STEPS + COMBINE2_AT
        at(s1, "fetch", 1, b)
        at(s1, "fetch_mixed", 1, b)
        for i in range(TOPK * CT):
            at(s1 + i // per, "gather", 1, b, i)
        for piece in range(len(pieces(1, b))):
            for part in range(6):
                at(start + (part if b < NB - 1 else part // 2) + 3 * piece, "combine", 1, b, part, piece)

    plan = [("xload", 0), ("norm", 0, 0), ("xn", 0, 0), ("xT", 0, 0, 0), ("xs", 0, 0), ("xT", 0, 0, 1), ("xs", 0, 1),
            ("conv", 0, 0), ("conv", 0, 1), ("thc", 0), ("xc", 0), ("dbl", 0), ("dtr", 0, 0), ("dtr", 0, 1),
            ("soft", 0), ("ln", 0), ("ct", 0), ("dt", 0)]
    plan += [("decay", 0)]
    running, waiting = [None, None], [None, None]
    fetched, tiled = [0, 0], [0, 0]

    def slot(lane, new, step):
        cur, out = running[lane], waiting[lane]
        if new is None and cur is None and out is None:
            return
        if cur is not None:
            plan.append(("gate", lane, cur))
        if new is not None:
            while fetched[lane] < min(new + 5, len(lanes[lane])) and avail[lanes[lane][fetched[lane]][:3]] <= step:
                plan.append(("tile", lane, fetched[lane]))
                fetched[lane] += 1
            first = None
            if tiled[lane] <= new:
                tiled[lane] = new + 1
                first = new
            ahead = None
            if fetched[lane] > new + 1:
                tiled[lane] = new + 2
                ahead = new + 1
            plan.append(("up", lane, new, first, ahead))
        if cur is not None or out is not None:
            plan.append(("flip", lane, cur, out))
        running[lane], waiting[lane] = new, cur

    for step in range(max(end + 3, max(extras) + 1)):
        q, n = divmod(step, NS)
        live = step < STEPS
        second = (step, 1) in starts
        order = AFTER_SCANS if step > STEPS else WITH_SECOND if second else WITH_ONE
        held = []
        for what in order:
            if what == "scan" and live:
                plan.append(("scan", step))
            elif what in ("a", "b", "c"):
                new = starts.get((step, 0), {}).get("ab".find(what)) if what != "c" else starts[step, 1][0]
                before_slot = len(plan)
                slot(1 if what == "b" else 0, new, step)
                if what.upper() in order and (what == "b" or running[0] is None or lanes[0][running[0]][0] == 1) and len(plan) > before_slot and plan[-1][0] == "flip":
                    held.append((what, plan.pop()))
            elif what in ("A", "B", "C"):
                for w, it in held:
                    if w == what.lower():
                        plan.append(it)
                held = [h for h in held if h[0] != what.lower()]
            elif what == "sum" and 0 < step <= STEPS:
                plan.append(("sum", step - 1))
                if n == 0:
                    plan.append(("accT", q - 1))
            elif what == "hflip":
                if step and n == 0 and step <= STEPS:
                    plan.append(("y", q - 1))
                if live:
                    plan.append(("hflip", step))
                if step and n == 0 and step <= STEPS:
                    plan.append(("mix_out", q - 1))
        assert not held
        plan += extras.get(step, [])
    return plan, lanes


def program(nc, T, out):
    plan, lanes = make_plan()

    use, flip_use = {}, {}

    def takes(*key):
        use[key] = len(use) + 1

    fronts, combos = [], []
    for it in plan:
        if it[0] in ("xT", "logits", "rank", "xs", "dbl", "ct", "dtr", "z", "mix_out", "gram", "pm", "wm", "attn"):
            takes(*it)
        elif it[0] == "flip":
            takes(*it)
            if it[2] is not None:
                flip_use[it[1], it[2]] = len(use)
        if it[0] == "norm":
            fronts.append(it[1:])
        if it[0] == "combine" and it[3:] == (0, 0):
            combos.append(it[1:3])
    front_no = {f: n + 1 for n, f in enumerate(fronts)}
    combo_no = {f: n for n, f in enumerate(combos)}
    pool_combo_no = {f: n for n, f in enumerate(f for f in combos if on_pool(*f))}
    pieces_before = [sum(len(pieces(*f)) for f in combos[:n]) for n in range(len(combos) + 1)]
    piece_no = {(*f, p): pieces_before[n] + p for n, f in enumerate(combos) for p in range(len(pieces(*f)))}
    gram_no = {f[1]: n + 1 for n, f in enumerate(f for f in fronts if f[0] == 1)}
    routed_before = {i: [sum(j[2] == "routed" for j in lanes[i][:k]) for k in range(len(lanes[i]) + 1)] for i in lanes}
    ends = {(i, j[:2]): k + 1 for i in lanes for k, j in enumerate(lanes[i])}
    mix_stores = [it for it in plan if it[0] in ("mix_out", "attn")]
    mix_no = {it: n for n, it in enumerate(mix_stores)}
    tile_ahead = {it[2]: routed_before[0][it[4]] + 1 for it in plan
                  if it[0] == "up" and it[1] == 0 and it[4] is not None and lanes[0][it[4]][2] == "routed"}
    wide_before = [sum(2 * HID[j[0], j[2]] > 512 for j in lanes[0][:k]) for k in range(len(lanes[0]) + 1)]
    carries = [sum((m // NS) % 2 == 0 for m in range(N + 1)) for N in range(STEPS)]

    with ExitStack() as ctx:
        def sb(name, shape, dt=F32):
            return ctx.enter_context(nc.sbuf_tensor(name, shape, dt))

        def ps(name, shape):
            return ctx.enter_context(nc.psum_tensor(name, shape, F32))

        def sem(name):
            return ctx.enter_context(nc.semaphore(name))

        w13a = sb("w13a", [P, NE, 2 * H0])
        w2a = sb("w2a", [P, NE, 3, P])
        w13s = sb("w13s", [P, 2 * S0])
        w2s = sb("w2s", [P, 2, P])
        w13b = sb("w13b", [P, NE + 1, 2 * H1])
        w2b = sb("w2b", [P, NE + 1, 2, P])
        w_in = sb("w_in", [P, 2 * DI])
        w_x = sb("w_x", [P, DK, R + 2 * NS])
        w_dt = sb("w_dt", [R, DI])
        w_out = sb("w_out", [P, DK, P])
        cw = sb("cw", [P, DK, 4])
        cb = sb("cb", [P, DK])
        bdt = sb("bdt", [P, DK])
        am = sb("am", [P, DK, NS])
        dpar = sb("dpar", [P, DK])
        gate = [sb("gate0", [P, NE]), sb("gate1", [P, NE + 1])]
        combi = sb("combi", [P, P])
        queryT = sb("queryT", [P, P])
        NCONST = 3 * P + NE + NE * CT + TILES + NE + NE * CT
        const = sb("const", [P, NCONST])
        ident, not_before, ones = (const[:, k * P:(k + 1) * P] for k in range(3))
        iota8 = const[:, 3 * P:3 * P + NE]
        steps128 = const[:, 3 * P + NE:3 * P + NE + NE * CT]
        tile_no = const[:, 3 * P + NE + NE * CT:3 * P + NE + NE * CT + TILES]
        last_at = 3 * P + NE + NE * CT + TILES
        mhalf = const[:, last_at:last_at + NE]
        goes_on = const[:, last_at + NE:NCONST]

        x = sb("x", [P, CT, P])
        xn = sb("xn", [P, CT, P])
        xnT = [[sb("xnT0", [P, L]), sb("xnT1", [P, L])], [sb("x1T", [P, L])] * 2]
        stats = sb("stats", [P, CT, 6])
        mv = sb("mv", [P, CT, 2])
        vpe = sb("vpe", [P, CT])
        rstd = sb("rstd", [P, CT])
        lg = sb("lg", [P, CT, NE + 1])
        mx = sb("mx", [P, CT])
        zl = sb("zl", [P, CT, NE])
        el = sb("el", [P, CT, NE])
        se = sb("se", [P, CT])
        pr = sb("pr", [P, CT, NE])
        top = sb("top", [P, CT, 8])
        idx = sb("idx", [P, CT, 8], U32)
        idf = sb("idf", [P, CT, 2])
        oh = sb("oh", [P, TOPK, CT, NE])
        picked = sb("picked", [P, NE, CT])
        sofar = sb("sofar", [P, NE * CT])
        rk = sb("rk", [P, (CT + 1) * NE])
        over = sb("over", [P, NE, CT])
        nt = sb("nt", [P, NE])
        incl = sb("incl", [P, NE])
        excl = sb("excl", [P, NE])
        slotf = sb("slotf", [P, CT, TOPK])
        cmp = sb("cmp", [P, TILES, NE])
        tef = sb("tef", [P, TILES])
        wts = [[sb(f"wts{l}{b}", [P, CT, TOPK]) for b in range(NB)] for l in range(2)]
        slots = [[sb(f"slots{l}{b}", [P, CT, TOPK], U32) for b in range(NB)] for l in range(2)]
        expert = [[sb(f"expert{l}{b}", [P, TILES], U32) for b in range(NB)] for l in range(2)]
        sg = sb("sg", [P, NB, CT])
        bd = sb("bd", [P, P])
        pm = sb("pm", [P, P])
        bdw = sb("bdw", [P, P])
        gy = sb("gy", [P, TOPK, CT, P])
        so = sb("so", [P, CT, P])
        sr = sb("sr", [P, CT, P])
        xr = sb("xr", [P, CT, P])
        s_st = sb("s_st", [P, HT, P])

        xs = sb("xs", [P, DK, HALF + 3])
        ca = sb("ca", [P, DK, HALF])
        v = sb("v", [P, DK, HALF])
        dbl = sb("dbl", [R + NS, HALF])
        zs = sb("zs", [P, DK, HALF])
        xc = [sb(f"xc{i}", [P, DK, HALF]) for i in range(2)]
        dt = [sb(f"dt{i}", [P, DK, HALF]) for i in range(2)]
        dtx = [sb(f"dtx{i}", [P, DK, HALF]) for i in range(2)]
        ct = sb("ct", [P, 2, HT, NS])
        bcb = sb("bcb", [P, 2, GB, HALF])
        dBx = sb("dBx", [P, 2, DK, HALF])
        h = sb("h", [P, 2, DK, HALF])
        carry = sb("carry", [P, DK, NS])
        acc = sb("acc", [P, HT, DI])
        y = sb("y", [P, DK, HALF])
        LW, YR = [H0, H1], 3
        xg = [sb(f"xg{i}", [P, 4, P]) for i in range(2)]
        xgT = [sb(f"xgT{i}", [P, P]) for i in range(2)]
        tj = [sb(f"tj{i}", [P, LW[i]]) for i in range(2)]
        hj = [sb(f"hj{i}", [P, 2, LW[i]]) for i in range(2)]
        hT = [sb(f"hT{i}", [P, (3 - i) * P]) for i in range(2)]
        yj = [sb(f"yj{i}", [P, YR, P]) for i in range(2)]

        def dram(name, shape):
            return nc.dram_tensor(name, shape, F32, kind="Internal").ap()

        b_rows = [dram(f"b_rows{q}", (NS, HALF)) for q in range(CH)]
        rows_in = [[dram(f"rows_in{l}{i}", (TILES * P, P)) for i in range(2)] for l in range(2)]
        rows_out = [[dram(f"rows_out{l}{b}", (YROWS, P)) for b in range(NB)] for l in range(2)]
        mixed = [[dram(f"mixed{l}{b}", (L, P)) for b in range(NB)] for l in range(2)]
        mid = [dram(f"mid{b}", (L, P)) for b in range(NB)]

        pA = ps("pA", [P, DK, HALF])
        pH = ps("pH", [P, 2, 512])
        pG = ps("pG", [P, 512])
        pU = ps("pU", [P, 512])
        p1 = ps("p1", [P, 512])
        pM = ps("pM", [P, 512])

        def gate_bank(i, k):
            return p1 if i == 1 else (pG, pU)[k % 2] if lanes[0][k][0] == 1 else pG

        def tile_bank(i, k):
            return p1 if i == 1 else (pG, pU)[k % 2] if lanes[0][k][0] == 1 else pU

        def gated_before(i, k):
            return k - 1 if i == 0 and k and lanes[0][k][0] == lanes[0][k - 1][0] == 1 else k

        def tj_of(i, k):
            hid = HID[lanes[i][k][0], lanes[i][k][2]]
            at = k % 2 * H1 if i == 0 and lanes[0][k][0] == 1 else 0
            return tj[i][:, at:at + hid]

        TA = 2 * H1
        YA = 3 * P

        mix_loaded, exp_loaded, zeroed, zero_tile = sem("mix_loaded"), sem("exp_loaded"), sem("zeroed"), sem("zero_tile")
        psum_cleared, scaled, decay_exp, prepared = sem("psum_cleared"), sem("scaled"), sem("decay_exp"), sem("prepared")
        bank_full, bank_read = sem("bank_full"), sem("bank_read")
        gate_full = sem("gate_full")
        x_in, stats_ready, ve_ready, rstd_ready, xn_ready = (
            sem("x_in"), sem("stats_ready"), sem("ve_ready"), sem("rstd_ready"), sem("xn_ready"))
        zl_ready, el_ready, picked_ready, slots_ready, sg_ready = (
            sem("zl_ready"), sem("el_ready"), sem("picked_ready"), sem("slots_ready"), sem("sg_ready"))
        scattered = [[sem(f"scattered{l}{i}") for i in range(2)] for l in range(2)]
        halo_ready, conv_ready, thc_ready, xc_ready = sem("halo_ready"), sem("conv_ready"), sem("thc_ready"), sem("xc_ready")
        rows_stored, act_chain, ln_ready, dt_ready, dtx_ready = (
            sem("rows_stored"), sem("act_chain"), sem("ln_ready"), sem("dt_ready"), sem("dtx_ready"))
        b_loaded = [sem("b_loaded0"), sem("b_loaded1")]
        y_ready, accT_full = sem("y_ready"), sem("accT_full")
        decay_ready, dBx_ready, h_ready, hflip_full, sum_done, carried = (
            sem("decay_ready"), sem("dBx_ready"), sem("h_ready"), sem("hflip_full"), sem("sum_done"), sem("carried"))
        mixed_stored, gathered, fetched, combined, mid_stored, out_stored = (
            sem("mixed_stored"), [sem("gathered0"), sem("gathered1")], sem("fetched"), sem("combined"), sem("mid_stored"),
            sem("out_stored"))
        rows_added = sem("rows_added")
        sum_ready, tg_ready, mixed_fetched, gathered_rest = sem("sum_ready"), sem("tg_ready"), sem("mixed_fetched"), sem("gathered_rest")
        dve_chain = sem("dve_chain")
        tile_in = [[sem(f"tile_in{i}{s}") for s in range(4)] for i in range(2)]
        tile_full, tile_copied = [sem(f"tile_full{i}") for i in range(2)], [sem(f"tile_copied{i}") for i in range(2)]
        gu_full, tanh_ready = [sem(f"gu_full{i}") for i in range(2)], [sem(f"tanh_ready{i}") for i in range(2)]
        a_ready, hj_ready = [sem(f"a_ready{i}") for i in range(2)], [sem(f"hj_ready{i}") for i in range(2)]
        out_rows = [[sem(f"out_rows{i}{s}") for s in range(YR)] for i in range(2)]

        block = ctx.enter_context(nc.Block())

        mix_loads = [
            (const[:], T["const"]),
            (w_in[:], T["L0_attn_W_in"]),
            (w_x[:], T["L0_attn_W_x"].rearrange("(k p) n -> p k n", p=P)),
            (w_dt[:], T["L0_attn_W_dt"]),
            (w_out[:], T["L0_attn_W_out"].rearrange("(k p) n -> p k n", p=P)),
            (cw[:], T["L0_attn_conv_w"].rearrange("(k p) j -> p k j", p=P)),
            (cb[:], T["conv_b"]), (bdt[:], T["b_dt"]), (dpar[:], T["D_param"]),
            (am[:], T["L0_attn_A_log"].rearrange("(k p) n -> p k n", p=P)),
            (gate[0][:], T["gate0T"]), (gate[1][:], T["gate1T"]),
            (combi[:], T["combi"]), (queryT[:], T["queryT"]),
        ]
        w1, w3, w2 = T["L0_ffn_w1"], T["L0_ffn_w3"], T["L0_ffn_w2"]
        v1, v3, v2 = T["L1_ffn_w_gate"], T["L1_ffn_w_up"], T["L1_ffn_w_down"]
        exp_loads = [
            (w13s[:, 0:S0], T["L0_ffn_sw1"]), (w13s[:, S0:2 * S0], T["L0_ffn_sw3"]),
            (w2s[:, 0, :], T["L0_ffn_sw2"][0:128, :]), (w2s[0:64, 1, :], T["L0_ffn_sw2"][128:192, :]),
            (w13a[:, :, 0:H0], w1.rearrange("e d h -> d e h")),
            (w13a[:, :, H0:2 * H0], w3.rearrange("e d h -> d e h")),
            (w2a[:, :, 0, :], w2[:, 0:128, :].rearrange("e h d -> h e d")),
            (w2a[:, :, 1, :], w2[:, 128:256, :].rearrange("e h d -> h e d")),
            (w2a[0:96, :, 2, :], w2[:, 256:352, :].rearrange("e h d -> h e d")),
            (w13b[:, 0:NE, 0:H1], v1.rearrange("e d h -> d e h")),
            (w13b[:, 0:NE, H1:2 * H1], v3.rearrange("e d h -> d e h")),
            (w13b[:, NE, 0:H1], T["L1_ffn_sw_gate"]), (w13b[:, NE, H1:2 * H1], T["L1_ffn_sw_up"]),
            (w2b[:, 0:NE, 0, :], v2[:, 0:128, :].rearrange("e h d -> h e d")),
            (w2b[0:48, 0:NE, 1, :], v2[:, 128:176, :].rearrange("e h d -> h e d")),
            (w2b[:, NE, 0, :], T["L1_ffn_sw_down"][0:128, :]), (w2b[0:48, NE, 1, :], T["L1_ffn_sw_down"][128:176, :]),
        ]
        by_tile = "(c p) d -> p c d"

        @block.sync
        def _(sp):
            for kind, *a in plan:
                if kind == "xload":
                    b, = a
                    if b:
                        sp.wait_ge(xn_ready, front_no[0, b - 1])
                    sp.dma_start(x[:], T["L0_attn_x"][b].rearrange(by_tile, p=P)).then_inc(x_in, 16)
                    if b == 0:
                        for dst, src in mix_loads:
                            sp.dma_start(dst, src).then_inc(mix_loaded, 16)
                        sp.wait_ge(zero_tile, 1)
                        for l in range(2):
                            for i in range(2):
                                rows = rows_in[l][i].rearrange(by_tile, p=P)
                                for c in range(0, TILES, CT):
                                    n = min(CT, TILES - c)
                                    sp.dma_start(rows[:, c:c + n, :], gy[:, 0, 0:n, :]).then_inc(zeroed, 16)
                            if l == 0:
                                for dst, src in exp_loads:
                                    sp.dma_start(dst, src).then_inc(exp_loaded, 16)
                elif kind == "dbl":
                    q, = a
                    sp.wait_ge(bank_read, use["dbl", q])
                    sp.dma_start(b_rows[q], dbl[R:R + NS, :]).then_inc(rows_stored, 16)
                elif kind == "tile":
                    i, k = a
                    l, b, what, t = lanes[i][k]
                    if what == "routed":
                        m = routed_before[i][k]
                        if m >= 4:
                            sp.wait_ge(tile_full[i], m - 3)
                        sp.wait_ge(scattered[l][b % 2], 16 * TOPK * CT * (b // 2 + 1))
                        sp.dma_start(xg[i][:, m % 4, :], rows_in[l][b % 2][t * P:(t + 1) * P, :]).then_inc(tile_in[i][m % 4], 16)
                elif kind == "flip" and a[2] is not None:
                    i, _, k = a
                    l, b, what, t = lanes[i][k]
                    sp.wait_ge(bank_read, use[(kind, *a)])
                    r = t if what == "routed" else TILES + t
                    sp.dma_start(rows_out[l][b][r * P:(r + 1) * P, :], yj[i][:, k % YR, :]).then_inc(out_rows[i][k % YR], 16)
                elif kind in ("mix_out", "attn"):
                    it = (kind, *a)
                    l, b, m = (0, a[0] // 2, a[0] % 2) if kind == "mix_out" else (1, a[0], a[1])
                    sp.wait_ge(bank_read, use[it])
                    sp.dma_start(mixed[l][b][m * HALF:(m + 1) * HALF, :].rearrange(by_tile, p=P), s_st[:]
                                 ).then_inc(mixed_stored, 16)
                elif kind == "fetch":
                    l, b = a
                    n = combo_no[l, b]
                    if n:
                        pl, pb = combos[n - 1]
                        sp.wait_ge(combined, pieces_before[n])
                        if pl == 0:
                            sp.wait_ge(xn_ready, front_no[1, pb])
                            sp.wait_ge(mid_stored, 16 * (pb + 1))
                        else:
                            sp.wait_ge(out_stored, 16 * (pb + 1))
                    for i in range(2):
                        if (i, (l, b)) in ends:
                            for r in range(min(YR, ends[i, (l, b)])):
                                sp.wait_ge(out_rows[i][r], 16 * ((ends[i, (l, b)] - r + YR - 1) // YR))
                    sp.dma_start(so[:], rows_out[l][b][TILES * P:, :].rearrange(by_tile, p=P)).then_inc(fetched, 16)
                    src = T["L0_attn_x"][b] if l == 0 else mid[b]
                    sp.dma_start(xr[:], src.rearrange(by_tile, p=P)).then_inc(fetched, 16)
                elif kind == "fetch_mixed":
                    l, b = a
                    final = mix_no[("mix_out", 2 * b + 1) if l == 0 else ("attn", b, 1)]
                    sp.wait_ge(mixed_stored, 16 * (final + 1))
                    sp.dma_start(sr[:], mixed[l][b].rearrange(by_tile, p=P)).then_inc(mixed_fetched, 16)
                elif kind == "combine" and a[2] == 5:
                    l, b, _, piece = a
                    c0, c1 = pieces(l, b)[piece]
                    sp.wait_ge(combined, piece_no[l, b, piece] + 1)
                    if l == 0:
                        sp.dma_start(mid[b].rearrange(by_tile, p=P), xr[:]).then_inc(mid_stored, 16)
                    else:
                        sp.dma_start(out[b].rearrange(by_tile, p=P)[:, c0:c1, :], xr[:, c0:c1, :]).then_inc(out_stored, 16)
            sp.wait_ge(out_stored, 16 * sum(len(pieces(1, b)) for b in range(NB)))

        @block.gpsimd
        def _(pool):
            for kind, *a in plan:
                if kind == "norm":
                    F = front_no[tuple(a)]
                    if F == 1:
                        pool.wait_ge(mix_loaded, 16 * len(mix_loads))
                    pool.wait_ge(stats_ready, F)
                    if F > 1:
                        pool.wait_ge(xn_ready, F - 1)
                    pool.tensor_scalar(vpe[:], mv[:, :, 1], EPS, None, ALU.add).then_inc(ve_ready, 1)
                    pool.wait_ge(ve_ready, F)
                    pool.tensor_tensor(rstd[:], vpe[:], mhalf, ALU.pow).then_inc(rstd_ready, 1)
                elif kind == "scatter":
                    l, b, i = a
                    c, k = divmod(i, TOPK)
                    if i == 0:
                        pool.wait_ge(slots_ready, front_no[l, b])
                        if b < 2:
                            pool.wait_ge(zeroed, 16 * 4 * ((TILES + CT - 1) // CT))
                        else:
                            for lane in range(2):
                                if (lane, (l, b - 2)) in ends:
                                    pool.wait_ge(tile_full[lane], routed_before[lane][ends[lane, (l, b - 2)]])
                    pool.indirect_dma_start(rows_in[l][b % 2], bass.IndirectOffsetOnAxis(ap=slots[l][b][:, c, k:k + 1], axis=0),
                                            xn[:, c, :], None).then_inc(scattered[l][b % 2], 16)
                elif kind == "gather":
                    l, b, i = a
                    c, k = divmod(i, TOPK)
                    n = combo_no[l, b]
                    if i == 0:
                        for lane in range(2):
                            if (lane, (l, b)) in ends:
                                for r in range(min(YR, ends[lane, (l, b)])):
                                    pool.wait_ge(out_rows[lane][r], 16 * ((ends[lane, (l, b)] - r + YR - 1) // YR))
                        if n:
                            pool.wait_ge(combined, pieces_before[n])
                    pool.indirect_dma_start(gy[:, k, c, :], None, rows_out[l][b],
                                            bass.IndirectOffsetOnAxis(ap=slots[l][b][:, c, k:k + 1], axis=0)
                                            ).then_inc(gathered[n % 2] if c < pieces(l, b)[0][1] else gathered_rest, 16)
                elif kind == "combine" and a[2] < 3 and on_pool(*a[:2]):
                    l, b, part, _ = a
                    n, m = combo_no[l, b], 3 * pool_combo_no[l, b]
                    if part == 0:
                        pool.wait_ge(gathered[n % 2], 16 * TOPK * CT * (n // 2 + 1))
                    if part < TOPK:
                        pool.tensor_tensor(gy[:, part], gy[:, part], wts[l][b][:, :, part:part + 1].broadcast_to([P, CT, P]), ALU.mult
                                           ).then_inc(rows_added, 1)
                    else:
                        pool.wait_ge(rows_added, m + TOPK)
                        pool.tensor_tensor(gy[:, 0], gy[:, 0], gy[:, 1], ALU.add).then_inc(rows_added, 1)
                elif kind in ("decay", "scan"):
                    N = 0 if kind == "decay" else a[0] + 1
                    if N == STEPS:
                        continue
                    q, n = divmod(N, NS)
                    G = N // GB
                    if n == 0:
                        pool.wait_ge(dtx_ready, q + 1)
                    if N % GB == 0:
                        pool.wait_ge(b_loaded[G % 2], 16 * (G // 2 + 1))
                    if N >= 2:
                        pool.wait_ge(h_ready, 2 * (N - 1))
                    row = bcb[:, G % 2, N % GB:N % GB + 1, :].broadcast_to([P, DK, HALF])
                    pool.tensor_tensor(dBx[:, N % 2], dtx[q % 2][:], row, ALU.mult).then_inc(dBx_ready, 1)

        @block.tensor
        def _(pe):
            mm = pe.matmul

            def take(*key):
                if use[key] > 1:
                    pe.wait_ge(bank_read, use[key] - 1)

            expert_reg = [[pe.alloc_register(f"expert{i}{j}") for j in range(4)] for i in range(2)]
            expert_of = [[None] * 4, [None] * 4]

            for kind, *a in plan:
                if kind == "xload" and a[0] == 0:
                    pe.wait_ge(mix_loaded, 16 * len(mix_loads))
                    pe.wait_ge(prepared, 1)
                elif kind == "xT":
                    l, b, m = a
                    pe.wait_ge(xn_ready, front_no[l, b])
                    take(*("xT", *a))
                    for c in range(4):
                        last = pe.transpose(pM[:, c * P:(c + 1) * P], xn[:, 4 * m + c, :], ident)
                    last.then_inc(bank_full, 1)
                elif kind == "logits":
                    l, b = a
                    take("logits", l, b)
                    for c in range(CT):
                        last = mm(pM[:, 16 * c:16 * c + NE + l], xnT[l][b % 2][:, c * P:(c + 1) * P], gate[l][:], start=True, stop=True)
                    last.then_inc(bank_full, 1)
                elif kind == "rank":
                    l, b = a
                    pe.wait_ge(picked_ready, front_no[l, b])
                    take("rank", l, b)
                    mm(pM[:, 0:CT * NE], ones, sofar[:], start=True, stop=False)
                    mm(pM[:, 0:CT * NE], not_before, picked[:].rearrange("p e c -> p (e c)"), start=False, stop=True)
                    last = mm(pM[:, CT * NE:(CT + 1) * NE], ones, sofar[:].rearrange("p (e c) -> p e c", c=CT)[:, :, CT - 1],
                              start=True, stop=True)
                    last.then_inc(bank_full, 1)
                elif kind == "gram":
                    take("gram", a[0])
                    for c in range(CT):
                        last = mm(pM[:, 0:P], xn[:, c, :], xn[:, c, :], start=(c == 0), stop=(c == CT - 1))
                    last.then_inc(bank_full, 1)
                elif kind == "pm":
                    take("pm", a[0])
                    mm(pM[:, 0:P], bd[:], combi[:], start=True, stop=True).then_inc(bank_full, 1)
                elif kind == "wm":
                    take("wm", a[0])
                    mm(pM[:, 0:P], queryT[:], pm[:], start=True, stop=True).then_inc(bank_full, 1)
                elif kind == "attn":
                    b, m = a
                    take("attn", b, m)
                    for c in range(4):
                        last = mm(pM[:, c * P:(c + 1) * P], xnT[1][0][:, (4 * m + c) * P:(4 * m + c + 1) * P], bdw[:], start=True, stop=True)
                    last.then_inc(bank_full, 1)
                elif kind in ("xs", "z"):
                    q, k = a
                    take(kind, q, k)
                    w = w_in[:, ((kind == "z") * DK + k) * P:((kind == "z") * DK + k + 1) * P]
                    mm(pM[:], w, xnT[0][q // 2 % 2][:, q % 2 * HALF:(q % 2 + 1) * HALF], start=True, stop=True).then_inc(bank_full, 1)
                elif kind == "dbl":
                    q, = a
                    pe.wait_ge(xc_ready, q + 1)
                    take("dbl", q)
                    for k in range(DK):
                        last = mm(pM[0:R + NS, :], w_x[:, k, 0:R + NS], xc[q % 2][:, k, :], start=(k == 0), stop=(k == DK - 1))
                    last.then_inc(bank_full, 1)
                elif kind == "ct":
                    q, = a
                    take("ct", q)
                    for c in range(HT):
                        for k in range(DK):
                            last = mm(pM[:, c * NS:(c + 1) * NS], xc[q % 2][:, k, c * P:(c + 1) * P], w_x[:, k, R + NS:],
                                      start=(k == 0), stop=(k == DK - 1))
                    last.then_inc(bank_full, 1)
                elif kind == "dtr":
                    q, k = a
                    if k == 0:
                        pe.wait_ge(bank_read, use["dbl", q])
                    take("dtr", q, k)
                    mm(pM[:], w_dt[:, k * P:(k + 1) * P], dbl[0:R, :], start=True, stop=True).then_inc(bank_full, 1)
                elif kind == "hflip":
                    N, = a
                    q, n = divmod(N, NS)
                    pe.wait_ge(h_ready, 2 * (N + 1))
                    if n == 0 and q:
                        pe.wait_ge(y_ready, q)
                    for half in range(2):
                        if N:
                            pe.wait_ge(sum_done, 2 * (N - 1) + half + 1)
                        for c in range(2):
                            for k in range(DK):
                                t = 2 * half + c
                                last = pe.transpose(pH[:, half, c * DI + k * P:c * DI + (k + 1) * P], h[:, N % 2, k, t * P:(t + 1) * P], ident)
                        last.then_inc(hflip_full, 1)
                elif kind == "accT":
                    q, = a
                    pe.wait_ge(sum_done, 2 * NS * (q + 1))
                    for k in range(DK):
                        for c in range(HT):
                            last = pe.transpose(pH[:, k, c * P:(c + 1) * P], acc[:, c, k * P:(k + 1) * P], ident)
                    last.then_inc(accT_full, 1)
                elif kind == "mix_out":
                    q, = a
                    pe.wait_ge(y_ready, q + 1)
                    take("mix_out", q)
                    for c in range(HT):
                        for k in range(DK):
                            last = mm(pM[:, c * P:(c + 1) * P], y[:, k, c * P:(c + 1) * P], w_out[:, k, :],
                                      start=(k == 0), stop=(k == DK - 1))
                    last.then_inc(bank_full, 1)
                elif kind == "up":
                    i, k, first, ahead = a
                    if k == 0:
                        pe.wait_ge(scaled, 1)
                    elif gated_before(i, k):
                        pe.wait_ge(hj_ready[i], gated_before(i, k))

                    def transpose_tile(j):
                        l, b, what, t = lanes[i][j]
                        m = routed_before[i][j]
                        pe.wait_ge(tile_in[i][m % 4], 16 * (m // 4 + 1))
                        pe.transpose(tile_bank(i, k)[:, TA:TA + P], xg[i][:, m % 4, :], ident).then_inc(tile_full[i], 1)
                        pe.wait_ge(slots_ready, front_no[l, b])
                        pe.reg_load(expert_reg[i][j % 4], expert[l][b][0:1, t:t + 1])
                        expert_of[i][j % 4] = pe.snap(expert_reg[i][j % 4], min_val=0, max_val=NE - 1)

                    l, b, what, t = lanes[i][k]
                    hid = HID[l, what]
                    if first is not None and what == "routed":
                        transpose_tile(first)
                    if what == "routed":
                        pe.wait_ge(tile_copied[i], routed_before[i][k] + 1)
                        tok = xgT[i][:]
                        e = expert_of[i][k % 4]
                        w = (w13a, w13b)[l][:, bass.ds(e, 1), :].rearrange("p o h -> p (o h)")
                    else:
                        tok = xnT[l][b % 2][:, t * P:(t + 1) * P]
                        w = w13s[:] if l == 0 else w13b[:, NE, :]
                    if 2 * hid > 512:
                        mm(pG[:, 0:hid], tok, w[:, 0:hid], start=True, stop=True).then_inc(gate_full, 1)
                        mm(pU[:, 0:hid], tok, w[:, hid:2 * hid], start=True, stop=True).then_inc(gu_full[i], 1)
                    else:
                        mm(gate_bank(i, k)[:, 0:2 * hid], tok, w, start=True, stop=True).then_inc(gu_full[i], 1)
                    if ahead is not None and lanes[i][ahead][2] == "routed":
                        transpose_tile(ahead)
                elif kind == "flip":
                    i, k, before_k = a
                    if k is not None:
                        pe.wait_ge(hj_ready[i], k + 1)
                    take(*("flip", *a))
                    if k is not None:
                        for m, w in enumerate(chunks(HID[lanes[i][k][0], lanes[i][k][2]])):
                            last = pe.transpose(pM[0:w, m * P:(m + 1) * P], hj[i][:, k % 2, m * P:m * P + w], ident)
                    if before_k is not None:
                        l, b, what, t = lanes[i][before_k]
                        ks = chunks(HID[l, what])
                        if what == "routed":
                            e = expert_of[i][before_k % 4]
                            w = (w2a, w2b)[l][:, bass.ds(e, 1), :, :].rearrange("p o k d -> p (o k) d")
                        else:
                            w = w2s[:] if l == 0 else w2b[:, NE, :, :]
                        for m, wd in enumerate(ks):
                            last = mm(pM[:, YA:YA + P], hT[i][0:wd, m * P:(m + 1) * P], w[0:wd, m, :],
                                      start=(m == 0), stop=(m == len(ks) - 1))
                    last.then_inc(bank_full, 1)

        @block.scalar
        def _(act):
            A = act.activation

            def decay(N):
                q, n = divmod(N, NS)
                if n == 0:
                    act.wait_ge(dt_ready, q + 1)
                for k in range(DK):
                    if N:
                        act.wait_ge(h_ready, 2 * (N - 1) + k + 1)
                    A(pA[:, k, :], dt[q % 2][:, k, :], ACT.Exp, scale=am[:, k, n:n + 1]).then_inc(decay_ready, 1)

            def b_group(G):
                q, g = divmod(G, NG)
                if g == 0:
                    act.wait_ge(rows_stored, 16 * (q + 1))
                if G >= 2:
                    act.wait_ge(dBx_ready, GB * (G - 1))
                src = b_rows[q][g * GB:(g + 1) * GB, :].rearrange("(o n) t -> o n t", o=1)
                act.dma_start(bcb[:, G % 2, :, :], src.broadcast_to([P, GB, HALF])).then_inc(b_loaded[G % 2], 16)

            for kind, *a in plan:
                if kind == "xload" and a[0] == 0:
                    act.wait_ge(mix_loaded, 16 * len(mix_loads))
                    A(am[:], am[:], ACT.Exp).then_inc(decay_exp, 1)
                    act.wait_ge(prepared, 1)
                elif kind == "xT":
                    l, b, m = a
                    act.wait_ge(bank_full, use["xT", l, b, m])
                    A(xnT[l][b % 2][:, m * 512:(m + 1) * 512], pM[:], ACT.Copy).then_inc(bank_read, 1)
                elif kind == "logits":
                    l, b = a
                    act.wait_ge(bank_full, use["logits", l, b])
                    if front_no[l, b] > 1:
                        act.wait_ge(zl_ready, front_no[l, b] - 1)
                    A(lg[:, :, 0:NE + l], pM[:, 0:16 * CT].rearrange("p (c e) -> p c e", e=16)[:, :, 0:NE + l], ACT.Copy
                      ).then_inc(bank_read, 1)
                elif kind == "rank":
                    l, b = a
                    act.wait_ge(bank_full, use["rank", l, b])
                    A(rk[:], pM[:, 0:(CT + 1) * NE], ACT.Copy).then_inc(bank_read, 1)
                elif kind == "gram":
                    b, = a
                    act.wait_ge(bank_full, use["gram", b])
                    for c in range(4):
                        r = slice(32 * c, 32 * c + 32)
                        last = A(bd[r, r], pM[r, r], ACT.Copy)
                    last.then_inc(bank_read, 1)
                elif kind == "top":
                    l, b = a
                    F = front_no[l, b]
                    act.wait_ge(zl_ready, F)
                    A(el[:], zl[:], ACT.Exp).then_inc(el_ready, 1)
                    if l == 1:
                        A(sg[:, b, :], lg[:, :, NE], ACT.Tanh, scale=0.5).then_inc(sg_ready, 1)
                elif kind == "pm":
                    b, = a
                    act.wait_ge(bank_full, use["pm", b])
                    A(pm[:], pM[:, 0:P], ACT.Copy).then_inc(bank_read, 1)
                elif kind == "wm":
                    b, = a
                    act.wait_ge(bank_full, use["wm", b])
                    for c in range(4):
                        r = slice(32 * c, 32 * c + 32)
                        last = A(bdw[r, r], pM[r, r], ACT.Copy)
                    last.then_inc(bank_read, 1)
                elif kind in ("attn", "mix_out"):
                    it = (kind, *a)
                    act.wait_ge(bank_full, use[it])
                    if mix_no[it]:
                        act.wait_ge(mixed_stored, 16 * mix_no[it])
                    A(s_st[:].rearrange("p c d -> p (c d)"), pM[:], ACT.Copy).then_inc(bank_read, 1)
                elif kind == "xs":
                    q, k = a
                    act.wait_ge(halo_ready, q + 1)
                    act.wait_ge(bank_full, use["xs", q, k])
                    if k == 0 and q:
                        act.wait_ge(dt_ready, q)
                    A(xs[:, k, 3:3 + HALF], pM[:], ACT.Copy)
                    A(ca[:, k, :], pM[:], ACT.Identity, scale=cw[:, k, 3:4], bias=cb[:, k:k + 1]).then_inc(bank_read, 1)
                elif kind == "thc":
                    q, = a
                    act.wait_ge(conv_ready, 2 * (q + 1))
                    if q:
                        act.wait_ge(dt_ready, q)
                    A(v[:], ca[:], ACT.Tanh).then_inc(thc_ready, 1)
                elif kind == "dbl":
                    q, = a
                    act.wait_ge(bank_full, use["dbl", q])
                    if q:
                        act.wait_ge(rows_stored, 16 * q)
                    A(dbl[:], pM[0:R + NS, :], ACT.Copy).then_inc(bank_read, 1)
                elif kind == "ct":
                    q, = a
                    act.wait_ge(bank_full, use["ct", q])
                    A(ct[:, q % 2, :, :].rearrange("p c n -> p (c n)"), pM[:, 0:HT * NS], ACT.Copy).then_inc(bank_read, 1)
                elif kind == "dtr":
                    q, k = a
                    if k == 0:
                        act.wait_ge(xc_ready, q + 1)
                    act.wait_ge(bank_full, use["dtr", q, k])
                    A(v[:, k, :], pM[:], ACT.Identity, bias=bdt[:, k:k + 1]).then_inc(bank_read, 1)
                elif kind == "soft":
                    q, = a
                    act.wait_ge(bank_read, use["dtr", q, 1])
                    A(ca[:], v[:], ACT.Abs).then_inc(act_chain, 1)
                    act.wait_ge(act_chain, 2 * q + 1)
                    A(ca[:], ca[:], ACT.Exp, scale=-1.0).then_inc(act_chain, 1)
                elif kind == "ln":
                    q, = a
                    act.wait_ge(act_chain, 2 * q + 2)
                    A(dt[q % 2][:], ca[:], ACT.Ln, bias=1.0).then_inc(ln_ready, 1)
                elif kind == "z":
                    q, k = a
                    act.wait_ge(bank_full, use["z", q, k])
                    if q:
                        act.wait_ge(y_ready, q)
                    A(zs[:, k, :], pM[:], ACT.Tanh, scale=0.5)
                    A(y[:, k, :], pM[:], ACT.Copy).then_inc(bank_read, 1)
                elif kind == "decay":
                    b_group(0)
                    b_group(1)
                    act.wait_ge(prepared, 2)
                    decay(0)
                elif kind == "scan":
                    N, = a
                    q, n = divmod(N, NS)
                    if N + 1 < STEPS:
                        decay(N + 1)
                    if N % GB == GB - 1 and N // GB + 2 < CH * NG:
                        b_group(N // GB + 2)
                    if q % 2 == 0:
                        act.wait_ge(h_ready, 2 * N + 2)
                        A(carry[:, :, n], h[:, N % 2, :, HALF - 1], ACT.Copy).then_inc(carried, 1)
                elif kind == "up":
                    i, k, first, ahead = a
                    l, b, what, t = lanes[i][k]
                    hid = HID[l, what]

                    def copy_tile(j):
                        act.wait_ge(tile_full[i], routed_before[i][j] + 1)
                        A(xgT[i][:], tile_bank(i, k)[:, TA:TA + P], ACT.Copy).then_inc(tile_copied[i], 1)

                    if first is not None and what == "routed":
                        copy_tile(first)
                    if 2 * hid > 512:
                        act.wait_ge(gate_full, wide_before[k] + 1)
                        A(tj_of(i, k), gate_bank(i, k)[:, 0:hid], ACT.Tanh).then_inc(tanh_ready[i], 1)
                    act.wait_ge(gu_full[i], k + 1)
                    if ahead is not None and lanes[i][ahead][2] == "routed":
                        copy_tile(ahead)
                    if 2 * hid <= 512:
                        A(tj_of(i, k), gate_bank(i, k)[:, 0:hid], ACT.Tanh).then_inc(tanh_ready[i], 1)
                elif kind == "flip":
                    i, k, before_k = a
                    act.wait_ge(bank_full, use[("flip", *a)])
                    if before_k is not None:
                        if before_k >= YR:
                            act.wait_ge(out_rows[i][before_k % YR], 16 * (before_k // YR))
                        last = A(yj[i][:, before_k % YR, :], pM[:, YA:YA + P], ACT.Copy)
                    if k is not None:
                        w = P * len(chunks(HID[lanes[i][k][0], lanes[i][k][2]]))
                        last = A(hT[i][:, 0:w], pM[:, 0:w], ACT.Copy)
                    last.then_inc(bank_read, 1)
                elif kind == "combine" and a[2] == 3:
                    l, b, _, piece = a
                    cs = slice(*pieces(l, b)[piece])
                    act.wait_ge(sum_ready, piece_no[l, b, piece] + 1)
                    A(gy[:, 1, cs], gy[:, 0, cs], ACT.Tanh, scale=0.5).then_inc(tg_ready, 1)

        @block.vector
        def _(dve):
            cnt = [0]

            def link(ins):
                cnt[0] += 1
                ins.then_inc(dve_chain, 1)
                dve.wait_ge(dve_chain, cnt[0])

            def per_token(ap, n):
                return ap.rearrange("p (c o) -> p c o", o=1).broadcast_to([P, CT, n])

            dve.memset(gy[:, 0], 0.0).then_inc(zero_tile, 1)
            for t in (pA, pH, pG, pU, p1, pM):
                dve.memset(t[:], 0.0)
            dve.memset(xs[:], 0.0)
            dve.memset(bd[:], 0.0)
            dve.memset(bdw[:], 0.0).then_inc(prepared, 1)
            dve.wait_ge(mix_loaded, 16 * len(mix_loads))
            dve.tensor_scalar(cw[:], cw[:], 0.5, None, ALU.mult)
            dve.tensor_scalar(cb[:], cb[:], 0.5, None, ALU.mult)
            dve.wait_ge(decay_exp, 1)
            dve.tensor_scalar(am[:], am[:], -1.0, None, ALU.mult).then_inc(prepared, 1)
            dve.wait_ge(prepared, 2)

            for kind, *a in plan:
                if kind == "norm":
                    l, b = a
                    F = front_no[l, b]
                    src = x if l == 0 else xr
                    if l == 0:
                        dve.wait_ge(x_in, 16 * (b + 1))
                    for c in range(CT):
                        last = dve.bn_stats(stats[:, c, :], src[:, c, :])
                    link(last)
                    for c in range(CT):
                        last = dve.bn_aggr(mv[:, c, :], stats[:, c, :])
                    last.then_inc(stats_ready, 1)
                elif kind == "xn":
                    l, b = a
                    F = front_no[l, b]
                    src = x if l == 0 else xr
                    dve.wait_ge(stats_ready, F)
                    dve.wait_ge(rstd_ready, F)
                    if F > 1:
                        pl, pb = fronts[F - 2]
                        dve.wait_ge(scattered[pl][pb % 2], 16 * TOPK * CT * (pb // 2 + 1))
                    for c in range(CT):
                        last = dve.tensor_scalar(xn[:, c, :], src[:, c, :], mv[:, c, 0:1], rstd[:, c:c + 1], ALU.subtract, ALU.mult)
                    last.then_inc(xn_ready, 1)
                elif kind == "top":
                    l, b = a
                    dve.wait_ge(bank_read, use["logits", l, b])
                    link(dve.tensor_reduce(mx[:], lg[:, :, 0:NE], op=ALU.max, axis=AX))
                    dve.tensor_tensor(zl[:], lg[:, :, 0:NE], per_token(mx[:], NE), ALU.subtract).then_inc(zl_ready, 1)
                elif kind == "route":
                    l, b = a
                    F = front_no[l, b]
                    dve.wait_ge(el_ready, F)
                    link(dve.tensor_reduce(se[:], el[:], op=ALU.add, axis=AX))
                    link(dve.reciprocal(se[:], se[:]))
                    link(dve.tensor_tensor(pr[:], el[:], per_token(se[:], NE), ALU.mult))
                    for c in range(CT):
                        last = dve.max(top[:, c, :], pr[:, c, :])
                    link(last)
                    for c in range(CT):
                        last = dve.max_index(idx[:, c, :], top[:, c, :], pr[:, c, :])
                    link(last)
                    link(dve.tensor_copy(idf[:], idx[:, :, 0:TOPK]))
                    io = iota8.rearrange("p (o e) -> p o e", o=1).broadcast_to([P, CT, NE])
                    for k in range(TOPK):
                        last = dve.tensor_tensor(oh[:, k], io, idf[:, :, k:k + 1].broadcast_to([P, CT, NE]), ALU.is_equal)
                    link(last)
                    link(dve.tensor_tensor(picked[:].rearrange("p e c -> p c e"), oh[:, 0], oh[:, 1], ALU.add))
                    dve.tensor_tensor_scan(sofar[:], goes_on, picked[:].rearrange("p e c -> p (e c)"), 0.0, ALU.mult, ALU.add
                                           ).then_inc(picked_ready, 1)
                    if l == 0:
                        link(dve.tensor_copy(wts[l][b][:], top[:, :, 0:TOPK]))
                    else:
                        link(dve.tensor_reduce(se[:], top[:, :, 0:TOPK], op=ALU.add, axis=AX))
                        link(dve.reciprocal(se[:], se[:]))
                        link(dve.tensor_tensor(wts[l][b][:], top[:, :, 0:TOPK], per_token(se[:], TOPK), ALU.mult))
                        dve.wait_ge(sg_ready, b + 1)
                        link(dve.tensor_scalar(sg[:, b, :], sg[:, b, :], 0.5, 0.5, ALU.mult, ALU.add))
                elif kind == "slots":
                    l, b = a
                    rank = rk[:, 0:CT * NE].rearrange("p (e c) -> p c e", c=CT)
                    dve.wait_ge(bank_read, use["rank", l, b])
                    link(dve.tensor_tensor(over[:], rk[:, CT * NE:].rearrange("p (e o) -> p e o", o=1).broadcast_to([P, NE, CT]),
                                           steps128.rearrange("p (e m) -> p e m", m=CT), ALU.is_gt))
                    link(dve.tensor_reduce(nt[:], over[:], op=ALU.add, axis=AX))
                    link(dve.tensor_tensor_scan(incl[:], ones[:, 0:NE], nt[:], 0.0, ALU.mult, ALU.add))
                    link(dve.tensor_tensor(excl[:], incl[:], nt[:], ALU.subtract))
                    link(dve.scalar_tensor_tensor(out=rank, in0=excl[:].rearrange("p (o e) -> p o e", o=1).broadcast_to([P, CT, NE]),
                                                  scalar=float(P), in1=rank, op0=ALU.mult, op1=ALU.add))
                    for k in range(TOPK):
                        link(dve.tensor_tensor(oh[:, k], oh[:, k], rank, ALU.mult))
                        last = dve.tensor_reduce(slotf[:, :, k], oh[:, k], op=ALU.add, axis=AX)
                    link(last)
                    link(dve.tensor_copy(slots[l][b][:], slotf[:]))
                    link(dve.tensor_tensor(cmp[:], tile_no.rearrange("p (j o) -> p j o", o=1).broadcast_to([P, TILES, NE]),
                                           incl[:].rearrange("p (o e) -> p o e", o=1).broadcast_to([P, TILES, NE]), ALU.is_ge))
                    link(dve.tensor_reduce(tef[:], cmp[:], op=ALU.add, axis=AX))
                    dve.tensor_scalar(expert[l][b][:], tef[:], float(NE - 1), None, ALU.min).then_inc(slots_ready, 1)
                elif kind == "xs":
                    q, k = a
                    if k == 0:
                        if q % 2 == 0:
                            dve.memset(xs[:, :, 0:3], 0.0).then_inc(halo_ready, 1)
                        else:
                            dve.tensor_copy(xs[:, :, 0:3], xs[:, :, HALF:HALF + 3]).then_inc(halo_ready, 1)
                elif kind == "conv":
                    q, k = a
                    dve.wait_ge(bank_read, use["xs", q, 1])
                    dve.wait_ge(halo_ready, q + 1)
                    for j in (2, 1, 0):
                        last = dve.scalar_tensor_tensor(out=ca[:, k, :], in0=xs[:, k, j:j + HALF], scalar=cw[:, k, j:j + 1],
                                                        in1=ca[:, k, :], op0=ALU.mult, op1=ALU.add)
                        if j:
                            link(last)
                    last.then_inc(conv_ready, 1)
                elif kind == "xc":
                    q, = a
                    dve.wait_ge(thc_ready, q + 1)
                    dve.wait_ge(conv_ready, 2 * q + 2)
                    dve.scalar_tensor_tensor(out=xc[q % 2][:], in0=v[:], scalar=1.0, in1=ca[:], op0=ALU.add, op1=ALU.mult
                                             ).then_inc(xc_ready, 1)
                elif kind == "dt":
                    q, = a
                    g = xs[:, :, 0:HALF]
                    dve.wait_ge(ln_ready, q + 1)
                    link(dve.tensor_scalar(g, ca[:], 1.0, None, ALU.add))
                    link(dve.scalar_tensor_tensor(out=g, in0=g, scalar=1.0, in1=ca[:], op0=ALU.subtract, op1=ALU.subtract))
                    link(dve.tensor_tensor(g, dt[q % 2][:], g, ALU.subtract))
                    dve.scalar_tensor_tensor(out=dt[q % 2][:], in0=v[:], scalar=0.0, in1=g, op0=ALU.max, op1=ALU.add
                                             ).then_inc(dt_ready, 1)
                    dve.wait_ge(dt_ready, q + 1)
                    dve.wait_ge(xc_ready, q + 1)
                    dve.tensor_tensor(dtx[q % 2][:], dt[q % 2][:], xc[q % 2][:], ALU.mult).then_inc(dtx_ready, 1)
                elif kind == "zsilu":
                    q, = a
                    dve.wait_ge(bank_read, use["z", q, 1])
                    link(dve.scalar_tensor_tensor(out=zs[:], in0=zs[:], scalar=1.0, in1=y[:], op0=ALU.add, op1=ALU.mult))
                elif kind == "scan":
                    N, = a
                    q, n = divmod(N, NS)
                    dve.wait_ge(dBx_ready, N + 1)
                    if N >= 2:
                        dve.wait_ge(hflip_full, 2 * (N - 1))
                        dve.wait_ge(carried, carries[N - 2])
                    if q % 2:
                        dve.wait_ge(carried, q // 2 * NS + n + 1)
                    for k in range(DK):
                        dve.wait_ge(decay_ready, 2 * N + k + 1)
                        dve.tensor_tensor_scan(h[:, N % 2, k, :], pA[:, k, :], dBx[:, N % 2, k, :],
                                               carry[:, k, n:n + 1] if q % 2 else 0.0, ALU.mult, ALU.add).then_inc(h_ready, 1)
                elif kind == "sum":
                    N, = a
                    q, n = divmod(N, NS)
                    if n == 0:
                        if q:
                            dve.wait_ge(accT_full, q)
                        dve.wait_ge(bank_read, use["ct", q])
                    for half in range(2):
                        dve.wait_ge(hflip_full, 2 * N + half + 1)
                        if n:
                            dve.wait_ge(sum_done, 2 * (N - 1) + half + 1)
                        for c in range(2):
                            t = 2 * half + c
                            src = pH[:, half, c * DI:(c + 1) * DI]
                            cn = ct[:, q % 2, t, n:n + 1]
                            if n == 0:
                                last = dve.tensor_scalar(acc[:, t, :], src, cn, None, ALU.mult)
                            else:
                                last = dve.scalar_tensor_tensor(out=acc[:, t, :], in0=src, scalar=cn, in1=acc[:, t, :],
                                                                op0=ALU.mult, op1=ALU.add)
                        last.then_inc(sum_done, 1)
                elif kind == "y":
                    q, = a
                    dve.wait_ge(accT_full, q + 1)
                    for k in range(DK):
                        last = dve.scalar_tensor_tensor(out=y[:, k, :], in0=xc[q % 2][:, k, :], scalar=dpar[:, k:k + 1], in1=pH[:, k, :],
                                                        op0=ALU.mult, op1=ALU.add)
                    link(last)
                    dve.scalar_tensor_tensor(out=y[:], in0=y[:], scalar=0.5, in1=zs[:], op0=ALU.mult, op1=ALU.mult).then_inc(y_ready, 1)
                elif kind == "tile":
                    if a[0] == 0 and a[1] == 0:
                        dve.wait_ge(exp_loaded, 16 * len(exp_loads))
                        dve.tensor_scalar(w13a[:, :, 0:H0], w13a[:, :, 0:H0], 0.5, None, ALU.mult)
                        dve.tensor_scalar(w13s[:, 0:S0], w13s[:, 0:S0], 0.5, None, ALU.mult)
                        dve.tensor_scalar(w13b[:, :, 0:H1], w13b[:, :, 0:H1], 0.5, None, ALU.mult).then_inc(scaled, 1)
                elif kind == "gate":
                    i, k = a
                    l, b, what, t = lanes[i][k]
                    hid = HID[l, what]
                    up = pU[:, 0:hid] if 2 * hid > 512 else gate_bank(i, k)[:, hid:2 * hid]
                    dve.wait_ge(tanh_ready[i], k + 1)
                    if k >= 2:
                        dve.wait_ge(bank_full, flip_use[i, k - 2])
                    dve.scalar_tensor_tensor(out=hj[i][:, k % 2, 0:hid], in0=tj_of(i, k), scalar=1.0, in1=gate_bank(i, k)[:, 0:hid],
                                             op0=ALU.add, op1=ALU.mult).then_inc(a_ready[i], 1)
                    dve.wait_ge(a_ready[i], k + 1)
                    if 2 * hid > 512:
                        dve.wait_ge(gu_full[i], k + 1)
                        if k in tile_ahead:
                            dve.wait_ge(tile_copied[i], tile_ahead[k])
                    dve.tensor_tensor(hj[i][:, k % 2, 0:hid], hj[i][:, k % 2, 0:hid], up, ALU.mult).then_inc(hj_ready[i], 1)
                elif kind == "combine":
                    l, b, part, piece = a
                    n, m = combo_no[l, b], piece_no[l, b, piece]
                    cs = slice(*pieces(l, b)[piece])
                    if l == 1 and part == piece == 0:
                        dve.wait_ge(fetched, 32 * (n + 1))
                        link(dve.tensor_tensor(so[:], so[:], per_token(sg[:, b, :], P), ALU.mult))
                    if on_pool(l, b) and part < TOPK:
                        continue
                    if part == 0:
                        if piece:
                            dve.wait_ge(gathered_rest, 16 * TOPK * (cs.stop - cs.start))
                        else:
                            dve.wait_ge(gathered[n % 2], 16 * TOPK * (CT * (n // 2) + cs.stop))
                    if part < TOPK:
                        link(dve.tensor_tensor(gy[:, part, cs], gy[:, part, cs], wts[l][b][:, cs, part:part + 1].broadcast_to([P, cs.stop - cs.start, P]),
                                               ALU.mult))
                    elif part == 2:
                        if not on_pool(l, b):
                            link(dve.tensor_tensor(gy[:, 0, cs], gy[:, 0, cs], gy[:, 1, cs], ALU.add))
                    elif part == 3:
                        dve.wait_ge(fetched, 32 * (n + 1))
                        if on_pool(l, b):
                            dve.wait_ge(rows_added, 3 * pool_combo_no[l, b] + 3)
                        dve.tensor_tensor(gy[:, 0, cs], gy[:, 0, cs], so[:, cs], ALU.add).then_inc(sum_ready, 1)
                    elif part == 4:
                        dve.wait_ge(tg_ready, m + 1)
                        dve.wait_ge(mixed_fetched, 16 * (n + 1))
                        link(dve.scalar_tensor_tensor(out=gy[:, 0, cs], in0=gy[:, 1, cs], scalar=1.0, in1=gy[:, 0, cs], op0=ALU.add, op1=ALU.mult))
                    else:
                        link(dve.tensor_tensor(gy[:, 0, cs], gy[:, 0, cs], sr[:, cs], ALU.mult))
                        dve.scalar_tensor_tensor(out=xr[:, cs], in0=gy[:, 0, cs], scalar=0.5, in1=xr[:, cs], op0=ALU.mult, op1=ALU.add
                                                 ).then_inc(combined, 1)
                        dve.wait_ge(combined, m + 1)


def kernel(**inputs):
    import numpy as np
    import concourse.bacc as bacc
    from concourse.bass_utils import run_bass_kernel_spmd

    def half(a):
        return np.ascontiguousarray(np.asarray(a).reshape(DK, P).T)

    nc = bacc.Bacc("TRN2", target_bir_lowering=False, num_devices=1)
    arrays = {n: np.ascontiguousarray(inputs[n]) for n in (
        "L0_attn_x", "L0_attn_W_in", "L0_attn_conv_w", "L0_attn_W_x", "L0_attn_W_dt", "L0_attn_A_log", "L0_attn_W_out",
        "L0_ffn_w1", "L0_ffn_w2", "L0_ffn_w3", "L0_ffn_sw1", "L0_ffn_sw2", "L0_ffn_sw3", "L1_ffn_w_gate", "L1_ffn_w_up",
        "L1_ffn_w_down", "L1_ffn_sw_gate", "L1_ffn_sw_up", "L1_ffn_sw_down")}
    arrays["conv_b"], arrays["b_dt"], arrays["D_param"] = (half(inputs["L0_attn_" + n]) for n in ("conv_b", "b_dt", "D_param"))
    arrays["gate0T"] = np.ascontiguousarray(np.asarray(inputs["L0_ffn_gate_w"]).T)
    arrays["gate1T"] = np.ascontiguousarray(
        np.concatenate([np.asarray(inputs["L1_ffn_gate_w"]), np.asarray(inputs["L1_ffn_shared_gate_w"])]).T)
    arrays["combi"] = np.ascontiguousarray(np.asarray(inputs["L1_attn_combiners"]).transpose(1, 0, 2).reshape(P, P))
    arrays["queryT"] = np.ascontiguousarray(np.asarray(inputs["L1_attn_queries"]).transpose(2, 0, 1).reshape(P, P))
    row = np.ones((P, 1), np.float32)
    arrays["const"] = np.ascontiguousarray(np.concatenate([
        np.eye(P), np.triu(np.ones((P, P)), 1) - 1, np.ones((P, P)), row * np.arange(NE), row * np.tile(P * np.arange(CT), NE),
        row * np.arange(TILES), row * np.full(NE, -0.5),
        row * np.tile(np.arange(CT) > 0, NE)], axis=1).astype(np.float32))
    T = {n: nc.dram_tensor(f"in_{n}", a.shape, mybir.dt.from_np(a.dtype), kind="ExternalInput").ap() for n, a in arrays.items()}
    out = nc.dram_tensor("out_0", (NB, L, P), F32, kind="ExternalOutput").ap()
    program(nc, T, out)
    r = run_bass_kernel_spmd(nc, [{f"in_{n}": a for n, a in arrays.items()}], core_ids=[0])
    return r.results[0]["out_0"]
```
